# Optimizing a Trainium2 kernel written in Bass

```python
import numpy as np
import jax
import jax.numpy as jnp

def _softmax(x, axis=-1):
    return jax.nn.softmax(x, axis=axis)

def _gelu(x):
    return jax.nn.gelu(x, approximate=True)

def _silu(x):
    return jax.nn.silu(x)

def _sigmoid(x):
    return jax.nn.sigmoid(x)

def _layernorm(x, axis=-1, eps=1e-05):
    m = jnp.mean(x, axis=axis, keepdims=True)
    v = jnp.var(x, axis=axis, keepdims=True)
    return (x - m) / jnp.sqrt(v + eps)

def _scatter_add(tgt, idx, src, axis=0):
    return tgt.at[idx].add(src)

def _segment_sum(src, seg, n):
    return jax.ops.segment_sum(src, seg, n)
kernel_name = 'mk_perceiver_d2_seqx_r4_2c8ace'

def setup_inputs(seed: int=0):
    np.random.seed(seed)
    _w = jnp.asarray

    def _rec_inputs():
        import jax
        import jax.numpy as jnp
        _rk = jax.random.key(seed)
        x = 7.22e-05 + 1 * jax.random.normal(jax.random.fold_in(_rk, 1), (1, 128, 256), jnp.float32)
        _lenS = 128 - jax.random.randint(jax.random.fold_in(_rk, 7), (1,), 0, max(1, 128 // 4) + 1, jnp.int32)
        _lenS2 = 12544 - jax.random.randint(jax.random.fold_in(_rk, 8), (1,), 0, max(1, 12544 // 4) + 1, jnp.int32)
        _ctx_768P = jax.random.normal(jax.random.fold_in(_rk, 11), (1, 16, 192), jnp.float32)
        _ctx_768c = jax.random.dirichlet(jax.random.fold_in(_rk, 511), 0.3 * jnp.ones((16,), jnp.float32), (1, 12544))
        _ctx_768t = jnp.einsum('bsk,bkd->bsd', _ctx_768c, _ctx_768P)
        _ctx_768t = _ctx_768t * jax.lax.rsqrt(jnp.mean(jnp.square(_ctx_768t)) + 1e-12) * 0.953939
        ctx_768 = -0.000191848 + 0.999787 * (_ctx_768t + 0.3 * jax.random.normal(jax.random.fold_in(_rk, 611), (1, 12544, 192), jnp.float32))
        _validS = jnp.arange(128)[None, :] < _lenS[:, None]
        _validS2 = jnp.arange(12544)[None, :] < _lenS2[:, None]
        _causal = jnp.tril(jnp.ones((128, 128), dtype=bool))
        mask_1x1xSxS2_bk0 = jnp.logical_not(jnp.broadcast_to(_validS2[0:1, None, None, :], (1, 1, 128, 12544)))
        return (x, ctx_768, mask_1x1xSxS2_bk0)
    x, ctx_768, mask_1x1xSxS2_bk0 = _rec_inputs()

    def _L0_xattn_setup():
        import jax, jax.numpy as jnp
        import numpy as np
        NUM_HEADS = 16
        CLAMP = 10000.0
        key = jax.random.key(seed)
        ks = jax.random.split(key, 8)
        B, Nq, Nkv, Cq, Ckv = (4, 512, 512, 256, 192)
        s_q = 1.0 / np.sqrt(Cq)
        s_kv = 1.0 / np.sqrt(Ckv)
        return {'query': jax.random.normal(ks[0], (B, Nq, Cq), jnp.float32), 'key_value': jax.random.normal(ks[1], (B, Nkv, Ckv), jnp.float32), 'Wq': jax.random.normal(ks[2], (Cq, Cq), jnp.float32) * s_q, 'bq': jnp.zeros((Cq,), jnp.float32), 'Wk': jax.random.normal(ks[3], (Ckv, Cq), jnp.float32) * s_kv, 'bk': jnp.zeros((Cq,), jnp.float32), 'Wv': jax.random.normal(ks[4], (Ckv, Cq), jnp.float32) * s_kv, 'bv': jnp.zeros((Cq,), jnp.float32), 'Wo': jax.random.normal(ks[5], (Cq, Cq), jnp.float32) * s_q, 'bo': jnp.zeros((Cq,), jnp.float32)}
    _L0_xattn_all = _L0_xattn_setup()
    _L0_xattn_in = {k: v for k, v in _L0_xattn_all.items() if k in ('Wq', 'bq', 'Wk', 'bk', 'Wv', 'bv', 'Wo', 'bo')}
    del _L0_xattn_all

    def _L0_attn_setup():
        import jax, jax.numpy as jnp
        import numpy as np
        import math
        B, T, D, M = (4, 512, 256, 64)
        key = jax.random.key(seed)
        ks = jax.random.split(key, 7)
        x = jax.random.normal(ks[0], (B, T, D), dtype=jnp.float32)
        Wk = jax.random.normal(ks[1], (M, D), dtype=jnp.float32) * math.sqrt(2.0 / M)
        Wv = jax.random.normal(ks[2], (M, D), dtype=jnp.float32) * math.sqrt(2.0 / M)
        Wq = jax.random.normal(ks[3], (M, D), dtype=jnp.float32) * math.sqrt(2.0 / M)
        Wg = jax.random.normal(ks[4], (1, D), dtype=jnp.float32) * math.sqrt(2.0 / 1)
        bg = jnp.array([1.0], dtype=jnp.float32)
        Wo = jax.random.normal(ks[5], (D, M), dtype=jnp.float32) * 0.01
        return {'x': x, 'Wk': Wk, 'Wv': Wv, 'Wq': Wq, 'Wg': Wg, 'bg': bg, 'Wo': Wo}
    _L0_attn_all = _L0_attn_setup()
    _L0_attn_in = {k: v for k, v in _L0_attn_all.items() if k in ('Wk', 'Wv', 'Wq', 'Wg', 'bg', 'Wo')}
    del _L0_attn_all

    def _L0_ffn_setup():
        import jax, jax.numpy as jnp
        import numpy as np
        EPS = 1e-05

        def _quantize(W):
            gamma = jnp.mean(jnp.abs(W))
            return jnp.clip(jnp.round(W / (gamma + EPS)), -1.0, 1.0)
        key = jax.random.key(seed)
        k_x, k_w1, k_b1, k_w2, k_b2 = jax.random.split(key, 5)
        n_embd = 256
        d_ff = 4 * n_embd
        B, S = (4, 1024)
        bound1 = 1.0 / np.sqrt(n_embd)
        bound2 = 1.0 / np.sqrt(d_ff)
        x = jax.random.normal(k_x, (B, S, n_embd), dtype=jnp.float32)
        W1 = jax.random.uniform(k_w1, (d_ff, n_embd), jnp.float32, -bound1, bound1)
        b1 = jax.random.uniform(k_b1, (d_ff,), jnp.float32, -bound1, bound1)
        W2 = jax.random.uniform(k_w2, (n_embd, d_ff), jnp.float32, -bound2, bound2)
        b2 = jax.random.uniform(k_b2, (n_embd,), jnp.float32, -bound2, bound2)
        return {'x': x, 'W1': W1, 'b1': b1, 'W2': W2, 'b2': b2}
    _L0_ffn_all = _L0_ffn_setup()
    _L0_ffn_in = {k: v for k, v in _L0_ffn_all.items() if k in ('W1', 'b1', 'W2', 'b2')}
    del _L0_ffn_all

    def _L1_xattn_setup():
        import jax, jax.numpy as jnp
        import numpy as np
        B, T, Q_DIM, KV_DIM = (4, 512, 256, 192)
        HEADS, DIM_HEAD = (16, 64)
        INNER = HEADS * DIM_HEAD
        NUM_FRAMES, NUM_PATCHES = (8, 64)
        LN_EPS = 1e-05

        def diagonal_frame_mask(num_patches, num_frames):
            fid = np.repeat(np.arange(num_frames), num_patches)
            m = fid[:, None] == fid[None, :]
            return jnp.asarray(m[None, None])
        key = jax.random.key(seed)
        ks = jax.random.split(key, 6)
        s = lambda d: 1.0 / np.sqrt(d)
        return {'x': jax.random.normal(ks[0], (B, T, Q_DIM), jnp.float32), 'context': jax.random.normal(ks[1], (B, T, KV_DIM), jnp.float32), 'ln_gamma': jnp.ones((Q_DIM,), jnp.float32), 'ln_beta': jnp.zeros((Q_DIM,), jnp.float32), 'Wq': jax.random.normal(ks[2], (Q_DIM, INNER), jnp.float32) * s(Q_DIM), 'Wkv': jax.random.normal(ks[3], (KV_DIM, 2 * INNER), jnp.float32) * s(KV_DIM), 'Wo': jax.random.normal(ks[4], (INNER, Q_DIM), jnp.float32) * s(INNER), 'bo': jnp.zeros((Q_DIM,), jnp.float32), 'mask': diagonal_frame_mask(NUM_PATCHES, NUM_FRAMES)}
    _L1_xattn_all = _L1_xattn_setup()
    _L1_xattn_in = {k: v for k, v in _L1_xattn_all.items() if k in ('ln_gamma', 'ln_beta', 'Wq', 'Wkv', 'Wo', 'bo')}
    del _L1_xattn_all

    def _L1_attn_setup():
        import jax, jax.numpy as jnp
        import numpy as np
        import math
        D_MODEL = 256
        N_HEAD = 16
        POWER = 2.0
        EPS = 1e-06

        def _alibi_slopes(n_head):
            closest = 2 ** math.floor(math.log2(n_head))
            base = 2 ** (-2 ** (-(math.log2(closest) - 3)))
            slopes = base ** np.arange(1, 1 + closest, dtype=np.float64)
            if closest != n_head:
                extra_base = 2 ** (-2 ** (-(math.log2(2 * closest) - 3)))
                num_rem = min(closest, n_head - closest)
                slopes = np.concatenate([slopes, extra_base ** np.arange(1, 1 + 2 * num_rem, 2, dtype=np.float64)])
            return jnp.asarray(slopes * 4.0, dtype=jnp.float32)
        key = jax.random.key(seed)
        ks = jax.random.split(key, 5)
        B, T, C = (2, 512, D_MODEL)
        x = jax.random.normal(ks[0], (B, T, C), dtype=jnp.float32)
        w_scale = 0.02
        Wq = jax.random.normal(ks[1], (C, C), dtype=jnp.float32) * w_scale
        Wk = jax.random.normal(ks[2], (C, C), dtype=jnp.float32) * w_scale
        Wv = jax.random.normal(ks[3], (C, C), dtype=jnp.float32) * w_scale
        Wo = jax.random.normal(ks[4], (C, C), dtype=jnp.float32) * w_scale
        alibi_slopes = _alibi_slopes(N_HEAD)
        power = jnp.full((1,), POWER, dtype=jnp.float32)
        return {'x': x, 'Wq': Wq, 'Wk': Wk, 'Wv': Wv, 'Wo': Wo, 'alibi_slopes': alibi_slopes, 'power': power}
    _L1_attn_all = _L1_attn_setup()
    _L1_attn_in = {k: v for k, v in _L1_attn_all.items() if k in ('Wq', 'Wk', 'Wv', 'Wo', 'alibi_slopes', 'power')}
    del _L1_attn_all

    def _L1_ffn_setup():
        import jax, jax.numpy as jnp
        import numpy as np
        IN_F = 256
        OUT_F = 256
        B, S = (8, 1024)

        def _pack_ternary(tern):
            enc = (tern + 1.0).astype(jnp.int32).reshape(-1)
            return (enc[0::4] | enc[1::4] << 2 | enc[2::4] << 4 | enc[3::4] << 6).astype(jnp.int32)
        key = jax.random.key(seed)
        kx, kw = jax.random.split(key)
        x = jax.random.normal(kx, (B, S, IN_F), dtype=jnp.float32)
        w = jax.random.normal(kw, (OUT_F, IN_F), dtype=jnp.float32) * 0.02
        scale = jnp.maximum(jnp.mean(jnp.abs(w)), 1e-05)
        wn = w / scale
        tern = jnp.sign(wn) * (jnp.abs(wn) > 0.5).astype(jnp.float32)
        packed = _pack_ternary(tern)
        bias = jnp.zeros((OUT_F,), dtype=jnp.float32)
        return {'x': x, 'packed_weight': packed, 'weight_scale': scale.reshape(1), 'bias': bias}
    _L1_ffn_all = _L1_ffn_setup()
    _L1_ffn_in = {k: v for k, v in _L1_ffn_all.items() if k in ('packed_weight', 'weight_scale', 'bias')}
    del _L1_ffn_all
    return {'x': x, 'ctx_768': ctx_768, 'mask_1x1xSxS2_bk0': mask_1x1xSxS2_bk0, 'L0_xattn_Wq': _L0_xattn_in['Wq'], 'L0_xattn_bq': _L0_xattn_in['bq'], 'L0_xattn_Wk': _L0_xattn_in['Wk'], 'L0_xattn_bk': _L0_xattn_in['bk'], 'L0_xattn_Wv': _L0_xattn_in['Wv'], 'L0_xattn_bv': _L0_xattn_in['bv'], 'L0_xattn_Wo': _L0_xattn_in['Wo'], 'L0_xattn_bo': _L0_xattn_in['bo'], 'L0_attn_Wk': _L0_attn_in['Wk'], 'L0_attn_Wv': _L0_attn_in['Wv'], 'L0_attn_Wq': _L0_attn_in['Wq'], 'L0_attn_Wg': _L0_attn_in['Wg'], 'L0_attn_bg': _L0_attn_in['bg'], 'L0_attn_Wo': _L0_attn_in['Wo'], 'L0_ffn_W1': _L0_ffn_in['W1'], 'L0_ffn_b1': _L0_ffn_in['b1'], 'L0_ffn_W2': _L0_ffn_in['W2'], 'L0_ffn_b2': _L0_ffn_in['b2'], 'L1_xattn_ln_gamma': _L1_xattn_in['ln_gamma'], 'L1_xattn_ln_beta': _L1_xattn_in['ln_beta'], 'L1_xattn_Wq': _L1_xattn_in['Wq'], 'L1_xattn_Wkv': _L1_xattn_in['Wkv'], 'L1_xattn_Wo': _L1_xattn_in['Wo'], 'L1_xattn_bo': _L1_xattn_in['bo'], 'L1_attn_Wq': _L1_attn_in['Wq'], 'L1_attn_Wk': _L1_attn_in['Wk'], 'L1_attn_Wv': _L1_attn_in['Wv'], 'L1_attn_Wo': _L1_attn_in['Wo'], 'L1_attn_alibi_slopes': _L1_attn_in['alibi_slopes'], 'L1_attn_power': _L1_attn_in['power'], 'L1_ffn_packed_weight': _L1_ffn_in['packed_weight'], 'L1_ffn_weight_scale': _L1_ffn_in['weight_scale'], 'L1_ffn_bias': _L1_ffn_in['bias']}

def reference(x, ctx_768, mask_1x1xSxS2_bk0, L0_xattn_Wq, L0_xattn_bq, L0_xattn_Wk, L0_xattn_bk, L0_xattn_Wv, L0_xattn_bv, L0_xattn_Wo, L0_xattn_bo, L0_attn_Wk, L0_attn_Wv, L0_attn_Wq, L0_attn_Wg, L0_attn_bg, L0_attn_Wo, L0_ffn_W1, L0_ffn_b1, L0_ffn_W2, L0_ffn_b2, L1_xattn_ln_gamma, L1_xattn_ln_beta, L1_xattn_Wq, L1_xattn_Wkv, L1_xattn_Wo, L1_xattn_bo, L1_attn_Wq, L1_attn_Wk, L1_attn_Wv, L1_attn_Wo, L1_attn_alibi_slopes, L1_attn_power, L1_ffn_packed_weight, L1_ffn_weight_scale, L1_ffn_bias):
    import jax
    import jax.numpy as jnp

    def _L0_xattn_ref(query, key_value, Wq, bq, Wk, bk, Wv, bv, Wo, bo):
        import jax, jax.numpy as jnp
        import numpy as np
        NUM_HEADS = 16
        CLAMP = 10000.0
        B, Nq, Cq = query.shape
        Nkv = key_value.shape[1]
        H = NUM_HEADS
        D = Cq // H
        scale = D ** (-0.5)
        q = (query @ Wq + bq).reshape(B, Nq, H, D).transpose(0, 2, 1, 3)
        k = (key_value @ Wk + bk).reshape(B, Nkv, H, D).transpose(0, 2, 1, 3)
        v = (key_value @ Wv + bv).reshape(B, Nkv, H, D).transpose(0, 2, 1, 3)
        attn = jnp.einsum('bhqd,bhkd->bhqk', q, k) * scale
        attn = jnp.clip(attn, -CLAMP, CLAMP)
        attn = jax.nn.softmax(attn, axis=-1)
        attn = jnp.where(jnp.any(jnp.isnan(attn)), jnp.asarray(1.0 / Nkv, attn.dtype), attn)
        x = jnp.einsum('bhqk,bhkd->bqhd', attn, v).reshape(B, Nq, Cq)
        return x @ Wo + bo

    def _L0_attn_ref(x, Wk, Wv, Wq, Wg, bg, Wo):
        import jax, jax.numpy as jnp
        import numpy as np
        import math
        B, T, D, M = (4, 512, 256, 64)
        Bb, Tt, Dd = x.shape
        Mm = Wk.shape[0]
        keys = x @ Wk.T
        vals = x @ Wv.T
        queries = x @ Wq.T
        gates = jax.nn.sigmoid(x @ Wg.T + bg)
        log_gates = jnp.log(gates[..., 0] + 1e-08)
        cum_log = jnp.cumsum(log_gates, axis=1)
        log_decay = cum_log[:, None, :] - cum_log[:, :, None]
        causal = jnp.triu(jnp.ones((Tt, Tt), dtype=x.dtype))
        decay = jnp.exp(jnp.minimum(log_decay, 0.0)) * causal
        scores = jnp.einsum('bim,bjm->bij', vals, queries) / math.sqrt(Mm)
        weighted = scores * decay
        reads = jnp.einsum('bij,bim->bjm', weighted, keys) / math.sqrt(Tt)
        return reads @ Wo.T

    def _L0_ffn_ref(x, W1, b1, W2, b2):
        import jax, jax.numpy as jnp
        import numpy as np
        EPS = 1e-05

        def _quantize(W):
            gamma = jnp.mean(jnp.abs(W))
            return jnp.clip(jnp.round(W / (gamma + EPS)), -1.0, 1.0)
        Wq1 = _quantize(W1)
        Wq2 = _quantize(W2)
        h = jax.nn.relu(jnp.einsum('bsd,fd->bsf', x, Wq1) + b1)
        out = jnp.einsum('bsf,df->bsd', h, Wq2) + b2
        return out

    def _L1_xattn_ref(x, context, ln_gamma, ln_beta, Wq, Wkv, Wo, bo, mask):
        import jax, jax.numpy as jnp
        import numpy as np
        B, T, Q_DIM, KV_DIM = (4, 512, 256, 192)
        HEADS, DIM_HEAD = (16, 64)
        INNER = HEADS * DIM_HEAD
        NUM_FRAMES, NUM_PATCHES = (8, 64)
        LN_EPS = 1e-05

        def diagonal_frame_mask(num_patches, num_frames):
            fid = np.repeat(np.arange(num_frames), num_patches)
            m = fid[:, None] == fid[None, :]
            return jnp.asarray(m[None, None])
        mu = jnp.mean(x, axis=-1, keepdims=True)
        var = jnp.mean(jnp.square(x - mu), axis=-1, keepdims=True)
        xn = (x - mu) * jax.lax.rsqrt(var + LN_EPS) * ln_gamma + ln_beta
        scale = DIM_HEAD ** (-0.5)
        q = xn @ Wq
        kv = context @ Wkv
        k, v = jnp.split(kv, 2, axis=-1)
        split_heads = lambda t: t.reshape(t.shape[0], t.shape[1], HEADS, DIM_HEAD).transpose(0, 2, 1, 3)
        q, k, v = (split_heads(q), split_heads(k), split_heads(v))
        dots = jnp.einsum('bhnd,bhmd->bhnm', q, k) * scale
        dots = jnp.where(mask, dots, -jnp.inf)
        attn = jax.nn.softmax(dots, axis=-1)
        out = jnp.einsum('bhnm,bhmd->bhnd', attn, v)
        out = out.transpose(0, 2, 1, 3).reshape(x.shape[0], x.shape[1], INNER)
        return out @ Wo + bo

    def _L1_attn_ref(x, Wq, Wk, Wv, Wo, alibi_slopes, power):
        import jax, jax.numpy as jnp
        import numpy as np
        import math
        D_MODEL = 256
        N_HEAD = 16
        POWER = 2.0
        EPS = 1e-06

        def _alibi_slopes(n_head):
            closest = 2 ** math.floor(math.log2(n_head))
            base = 2 ** (-2 ** (-(math.log2(closest) - 3)))
            slopes = base ** np.arange(1, 1 + closest, dtype=np.float64)
            if closest != n_head:
                extra_base = 2 ** (-2 ** (-(math.log2(2 * closest) - 3)))
                num_rem = min(closest, n_head - closest)
                slopes = np.concatenate([slopes, extra_base ** np.arange(1, 1 + 2 * num_rem, 2, dtype=np.float64)])
            return jnp.asarray(slopes * 4.0, dtype=jnp.float32)
        B, T, C = x.shape
        H = N_HEAD
        Dh = C // H
        Q = (x @ Wq.T).reshape(B, T, H, Dh).transpose(0, 2, 1, 3)
        K = (x @ Wk.T).reshape(B, T, H, Dh).transpose(0, 2, 1, 3)
        V = (x @ Wv.T).reshape(B, T, H, Dh).transpose(0, 2, 1, 3)
        scale = 1.0 / Dh ** 0.5 * 16.0
        scores = jnp.einsum('bhqd,bhkd->bhqk', Q, K) * scale
        idx = jnp.arange(T, dtype=jnp.float32)
        distance = idx[None, :] - idx[:, None]
        scores = scores - alibi_slopes[None, :, None, None] * jnp.abs(distance)[None, None]
        scores = jnp.where(distance[None, None] > 0, jnp.float32(-10000.0), scores)
        s = scores / (jnp.abs(scores) + 1.0)
        p = ((s + 1.0) * 0.5) ** power[0]
        probs = p / (p.sum(axis=-1, keepdims=True) + EPS)
        out = jnp.einsum('bhqk,bhkd->bhqd', probs, V)
        out = out.transpose(0, 2, 1, 3).reshape(B, T, C)
        return out @ Wo.T

    def _L1_ffn_ref(x, packed_weight, weight_scale, bias):
        import jax, jax.numpy as jnp
        import numpy as np
        IN_F = 256
        OUT_F = 256
        B, S = (8, 1024)

        def _pack_ternary(tern):
            enc = (tern + 1.0).astype(jnp.int32).reshape(-1)
            return (enc[0::4] | enc[1::4] << 2 | enc[2::4] << 4 | enc[3::4] << 6).astype(jnp.int32)
        n = OUT_F * IN_F
        shifts = jnp.array([0, 2, 4, 6], dtype=jnp.int32)
        enc = (packed_weight[None, :] >> shifts[:, None] & 3).reshape(-1)[:n]
        w = (enc.astype(jnp.float32) - 1.0).reshape(OUT_F, IN_F) * weight_scale
        act_scale = 127.0 / jnp.maximum(jnp.max(jnp.abs(x), axis=-1, keepdims=True), 1e-05)
        x_dq = jnp.clip(jnp.round(x * act_scale), -128.0, 127.0) / act_scale
        return jnp.einsum('bsi,oi->bso', x_dq, w) + bias
    x = x + _L0_xattn_ref(_layernorm(x, axis=-1), ctx_768, L0_xattn_Wq, L0_xattn_bq, L0_xattn_Wk, L0_xattn_bk, L0_xattn_Wv, L0_xattn_bv, L0_xattn_Wo, L0_xattn_bo)
    x = x + _L0_attn_ref(_layernorm(x, axis=-1), L0_attn_Wk, L0_attn_Wv, L0_attn_Wq, L0_attn_Wg, L0_attn_bg, L0_attn_Wo)
    x = x + _L0_ffn_ref(_layernorm(x, axis=-1), L0_ffn_W1, L0_ffn_b1, L0_ffn_W2, L0_ffn_b2)
    x = x + _L1_xattn_ref(_layernorm(x, axis=-1), ctx_768, L1_xattn_ln_gamma, L1_xattn_ln_beta, L1_xattn_Wq, L1_xattn_Wkv, L1_xattn_Wo, L1_xattn_bo, mask_1x1xSxS2_bk0)
    x = x + _L1_attn_ref(_layernorm(x, axis=-1), L1_attn_Wq, L1_attn_Wk, L1_attn_Wv, L1_attn_Wo, L1_attn_alibi_slopes, L1_attn_power)
    x = x + _L1_ffn_ref(_layernorm(x, axis=-1), L1_ffn_packed_weight, L1_ffn_weight_scale, L1_ffn_bias)
    return x

_drawn_inputs = setup_inputs


def setup_inputs(seed=0):
    import zlib

    import numpy as np

    out = dict(_drawn_inputs(seed))
    spreads = {'L0_xattn_bq': (0.0, 0.388),
     'L0_xattn_bk': (0.0, 2.0),
     'L0_xattn_bv': (0.0, 0.1),
     'L0_xattn_bo': (0.0, 0.1),
     'L1_xattn_ln_gamma': (1.0, 0.6),
     'L1_xattn_ln_beta': (0.0, 0.8),
     'L1_xattn_bo': (0.0, 2.0),
     'L1_ffn_bias': (0.0, 2.0)}
    factors = {'L0_ffn_b1': 8.0,
     'L0_ffn_b2': 200.0,
     'L1_xattn_Wq': 8.0,
     'L1_xattn_Wkv': 8.0,
     'L1_xattn_Wo': 8.0,
     'L1_attn_Wq': 64.0,
     'L1_attn_Wk': 64.0,
     'L1_attn_Wv': 34.693,
     'L1_attn_Wo': 32.995,
     'L1_attn_alibi_slopes': 64.0}
    for name, (base, spread) in spreads.items():
        noise = np.random.default_rng([zlib.crc32(name.encode()), seed]).standard_normal(out[name].shape)
        drawn = base * np.exp(spread * noise) if base else spread * noise
        out[name] = jnp.asarray(drawn.astype(out[name].dtype))
    for name, factor in factors.items():
        out[name] = (out[name] * factor).astype(out[name].dtype)
    return out
```

```python
from contextlib import ExitStack

import numpy as np

import concourse.bass as bass
from concourse import mybir

F32 = mybir.dt.float32
F32R = mybir.dt.float32r
BF16 = mybir.dt.bfloat16
I32 = mybir.dt.int32
U8 = mybir.dt.uint8
ALU = mybir.AluOpType
ACT = mybir.ActivationFunctionType
AX_X = mybir.AxisListType.X
AX_XY = mybir.AxisListType.XY

P = 128
T = 128
C = 256
CKV = 192
S2 = 12544
H = 16
HQ = H * T
D0 = C // H
D1 = 64
INNER = H * D1
M0 = 64
FF = 4 * C
CH = 896
NCH = S2 // CH
TPC = CH // P
NB = CH // 2
HALVES = 2 * TPC
GROUPS = H // 2
NSUP = NCH // 2
CLAMP = 10000.0
EPS_LN = 1e-5
BIG = 1.0e30

K_ID, K_TRI, K_ONE, K_DIST, K_SEL, K_HEAD = 0, 128, 256, 384, 512, 640
K_END = 648

R_BV0, R_BO0, R_B2, R_GAM, R_BET, R_BO1, R_FB = range(7)

W_AH, W_AL, W_BH, W_BL = range(4)
X_AH, X_AL, X_B = range(3)
PAIRS = [(W_AH, X_AH), (W_AL, X_AH), (W_AH, X_AL), (W_BH, X_B), (W_BL, X_B)]

KEYS_AT = [0, 2, 4, 6]
VALUES_AT = [1, 3, 5, 7, 8, 9, 11]
K_ORDER = [1 + sorted(KEYS_AT + VALUES_AT).index(u) for u in KEYS_AT]
V_ORDER = [1 + sorted(KEYS_AT + VALUES_AT).index(u) for u in VALUES_AT]


TURNS = ["x0", "o0", "x1", "x2", "x3", "x4", "o4", "x5"]


def turn(tag):
    return TURNS.index(tag) + 1


class Signals(dict):

    def __init__(self, nc, ctx):
        super().__init__()
        self.nc, self.ctx = nc, ctx

    def __missing__(self, name):
        self[name] = self.ctx.enter_context(self.nc.semaphore(name))
        return self[name]


def perceiver(nc, a, out):
    with ExitStack() as ctx:
        S = Signals(nc, ctx)

        def sb(name, shape, dt=F32):
            return ctx.enter_context(nc.sbuf_tensor(name, shape, dt))

        ps = ctx.enter_context(nc.psum_tensor("ps", [P, 8, 512], F32))

        raw = sb("raw", [P, 2, CH])
        ct = sb("ct", [P, 2, 3, CH], F32R)
        hi_tmp = sb("hi_tmp", [P, CH], F32R)
        khl = sb("khl", [P, 2, 2, CH], F32R)
        ks = sb("ks", [P, 2 * GROUPS * CH], F32R)
        ks_v = ks[:, :].rearrange("p (b g n) -> p b g n", b=2, g=GROUPS)
        qs = sb("qs", [P, HQ], F32R)
        nm = sb("nm", [P, HQ])
        v17 = sb("v17", [P, 2 * TPC * H * 17])
        v17_v = v17[:, :].rearrange("p (b t h d) -> p b t h d", b=2, t=TPC, h=H)
        pr = sb("pr", [P, 4, 1024])
        pr_flat = pr[:, :, :].rearrange("p s n -> p (s n)")
        wk0 = sb("wk0", [P, 4, C], F32R)
        wv0 = sb("wv0", [P, 4, C], F32R)
        ffw = sb("ffw", [P, 4096])
        wraw = sb("wraw", [P, 2, 2, C])
        qn = ks[:, 0:HQ].rearrange("p (h q) -> p h q", h=H)
        kn = ks[:, HQ:HQ + 4 * CH].rearrange("p (b t n) -> p b t n", b=2, t=2)
        asp = ks[:, 0:4 * HQ].rearrange("p (w n) -> p w n", w=4)
        wv1 = ks[:, 4 * HQ:4 * HQ + 4 * INNER].rearrange("p (w n) -> p w n", w=4)
        x5 = khl[:, 0, :, :]
        kabs = nm[:, 0:2 * CH].rearrange("p (t n) -> p t n", t=2)
        ksq = pr_flat[:, 2048:2048 + 2 * CH].rearrange("p (t n) -> p t n", t=2)
        con = sb("con", [P, K_END])
        rows = sb("rows", [P, 7, C])
        x = sb("x", [P, C])
        xn = sb("xn", [P, C])
        xnT = sb("xnT", [P, 2, T])
        wq0 = sb("wq0", [P, 3, C])
        bk0 = sb("bk0", [P, 2])
        wo0 = sb("wo0", [P, 2, C])
        zero = sb("zero", [P, 512], BF16)
        selr = sb("selr", [P, P], F32R)
        neg = sb("neg", [P, T])
        st6 = sb("st6", [P, 6])
        mv = sb("mv", [P, 2])
        rstd = sb("rstd", [P, 1])
        expo = sb("expo", [P, 3])
        cm = sb("cm", [P, H])
        mx = sb("mx", [P, H])
        mhi = sb("mhi", [P, H], F32R)
        ml = sb("ml", [P, H, 32])
        qabs = sb("qabs", [P, 2])
        kmax = sb("kmax", [P, 2])
        bound = sb("bound", [P, 2])
        bsum = sb("bsum", [P, 1])
        clipf = sb("clipf", [1, 1], I32)
        cnt = sb("cnt", [P, 8])
        cf = sb("cf", [1, 3, 8])
        sup = sb("sup", [1, 2, 8], I32)
        wsum = sb("wsum", [P, 2])
        thr = sb("thr", [P, 4])
        oacc = sb("oacc", [P, 4, T])
        pause = sb("pause", [P, 4])
        rl = sb("rl", [P, H])
        on = sb("on", [P, C])
        onT = sb("onT", [P, 2, T])
        a0w = sb("a0w", [P, 2, 3 * M0 + 1])
        a0wo = sb("a0wo", [M0, C])
        nbg = sb("nbg", [P, 1])
        g1 = sb("g1", [P, 4])
        b1c = sb("b1c", [P, FF // P])
        slp = sb("slp", [P, H + 1])
        fsc = sb("fsc", [P, 1])
        pk = sb("pk", [P, 2, 64], I32)
        ffw1 = ffw[:, 0:2048].rearrange("p (k n) -> p k n", k=2)
        ffw2 = ffw[:, 2048:4096].rearrange("p (k n) -> p k n", k=8)
        wo1 = ffw[:, 0:2048].rearrange("p (k n) -> p k n", k=8)
        aw = ffw[:, 2048:4096].rearrange("p (w k n) -> p w k n", w=4, k=2)
        wqp = pr_flat.rearrange("p (k n) -> p k n", k=2)
        wqp_b = ffw[0:1, 0:HQ]
        wq1 = pr_flat[:, 0:2048].rearrange("p (k n) -> p k n", k=2)
        wkt = pr_flat[:, 2048:4096].rearrange("p (k n) -> p k n", k=8)
        negm = pr_flat[:, 0:2 * CH].rearrange("p (b n) -> p b n", b=2)
        junk = pr_flat[:, 2 * CH:3 * CH]
        wv1raw = v17[:, 0:2048].rearrange("p (k n) -> p k n", k=2)
        v1 = v17[:, 0:2048].rearrange("p (b n) -> p b n", b=2)
        q1 = v17[:, 2048:2048 + INNER]
        enc = wq0[:, 0, 0:2 * 64].bitcast(I32).rearrange("p (k n) -> p k n", k=2)
        wtf = wq0[:, 1:3, :]
        mk4 = wraw[:, 0, :, :].rearrange("p k n -> p (k n)")[:, 0:2 * CH // 4].bitcast(I32)
        mq4 = wraw[:, 1, :, :].rearrange("p k n -> p (k n)")[:, 0:2 * CH // 4].bitcast(I32)
        mflat4 = v17[:, 0:S2 // 4].bitcast(I32)
        mk = mk4.bitcast(U8).rearrange("p (b t q) -> p b t q", b=2, t=TPC)
        mq = mq4.bitcast(U8).rearrange("p (b n) -> p b n", b=2)
        mflat = mflat4.bitcast(U8)

        ident = con[:, K_ID:K_ID + P]
        tri = con[:, K_TRI:K_TRI + P]
        ones = con[:, K_ONE:K_ONE + P]
        dist = con[:, K_DIST:K_DIST + P]
        headsel = con[:, K_HEAD:K_HEAD + 8]

        def bank(b, n=1):
            return ps[:, b:b + n, :].rearrange("p b n -> p (b n)")

        def lo_rows(k):
            return k.rearrange("p (g e s f d) -> p g e s f d", g=GROUPS, e=2, s=4, f=2)

        ctx_t = a["ctxT"]

        block = ctx.enter_context(nc.Block())

        @block.sync
        def _(sp):
            def load(dst, src, name):
                sp.dma_start(dst, src).then_inc(S[name], 16)

            def carry_wait():
                sp.sem_inc(S["carried"], 1)

            load(x[:, :], a["x"], "ld_x")
            load(con[:, :], a["constants"], "ld_con")
            load(wq0[:, 0:2, :], a["Wq0"].rearrange("(k p) n -> p k n", k=2), "ld_wq0")
            load(wq0[0:1, 2, :], a["bq0"], "ld_wq0")
            load(wraw[:, 0, :, :], a["Wk0"].rearrange("(k p) n -> p k n", k=2), "ld_wkv0")
            load(wraw[:, 1, :, :], a["Wv0"].rearrange("(k p) n -> p k n", k=2), "ld_wkv0")
            load(bk0[:, :], a["bk0"], "ld_wkv0")

            def load_max0(c, first):
                if not first:
                    sp.wait_ge(S["m0_split"], c)
                load(raw[:, 0, :], ctx_t[0:P, bass.ds(c * CH, CH)], "m0_raw")
                load(raw[0:64, 1, :], ctx_t[P:CKV, bass.ds(c * CH, CH)], "m0_raw")

            load_max0(0, True)
            load(mflat4, a["mask_q"], "ld_mask")
            for r, name in ((R_BV0, "bv0"), (R_BO0, "bo0"), (R_B2, "b2"), (R_GAM, "gamma"),
                            (R_BET, "beta"), (R_BO1, "bo1"), (R_FB, "fbias")):
                load(rows[:, r, :], a[name].partition_broadcast(P).rearrange("p o n -> p (o n)"), "ld_rows")
            load(wo0[:, :, :], a["Wo0"].rearrange("(k p) n -> p k n", k=2), "ld_small")
            load(a0w[:, :, :], a["A0"].rearrange("(k p) n -> p k n", k=2), "ld_small")
            load(a0wo[:, :], a["A0o"], "ld_small")
            load(nbg[:, :], a["bg"].partition_broadcast(P).rearrange("p o n -> p (o n)"), "ld_small")
            load(b1c[:, :], a["b1"], "ld_small")
            load(slp[:, 0:H], a["slopes"].partition_broadcast(P).rearrange("p o n -> p (o n)"), "ld_small")
            load(slp[:, H:H + 1], a["power"].partition_broadcast(P).rearrange("p o n -> p (o n)"), "ld_small")
            load(fsc[:, :], a["fscale"].partition_broadcast(P).rearrange("p o n -> p (o n)"), "ld_small")
            load(pk[:, :, :], a["packed"].rearrange("(k p) n -> p k n", k=2), "ld_small")
            load_max0(1, False)
            sp.wait_ge(S["qs_hi"], 1)
            sp.wait_ge(S["mask_sum"], NSUP)
            load(ffw1, a["W1T"].rearrange("(k p) n -> p k n", k=2), "ld_ffw")
            load(ffw2, a["W2T"].rearrange("(k p) n -> p k n", k=8), "ld_ffw")

            with sp.Fori(2, NCH) as c:
                load_max0(c, False)

            def load_sum0(c):
                sp.wait_ge(S["e0_hi"], c + 1)
                sp.wait_ge(S["e0_lo"], c + 1)
                load(raw[:, 0, :], ctx_t[0:P, bass.ds(c * CH, CH)], "e0_raw")
                load(raw[0:64, 1, :], ctx_t[P:CKV, bass.ds(c * CH, CH)], "e0_raw")
                load(raw[64:P, 1, :], ctx_t[P:CKV, bass.ds(c * CH, CH)], "e0_raw")

            def stack_keys(c, b):
                sp.wait_ge(S["e0_klo"], 4 * c + 6)
                carry_wait()
                sp.wait_ge(S["e0_score"], HALVES * (c + 1))
                for slot, part in ((0, 0), (1, 0), (2, 1)):
                    for g in range(4):
                        sp.dma_start(ks_v[32 * slot:32 * slot + 32, b, g::4, :].bitcast(F32),
                                     khl[32 * g:32 * g + 32, part, :, :].bitcast(F32)
                                     ).then_inc(S[f"e0_keys{b}"], 16)

            sp.wait_ge(S["m0_split"], NCH)
            load_sum0(0)
            with sp.Fori(0, NCH - 2, 2) as c:
                for b in range(2):
                    load_sum0(c + b + 1)
                    stack_keys(c + b, b)
            load_sum0(NCH - 1)
            stack_keys(NCH - 2, 0)
            stack_keys(NCH - 1, 1)

            sp.wait_ge(S["o0_read"], 1)
            load(wq1, a["Wq1"].rearrange("(k p) n -> p k n", k=2), "ld_w1")
            load(wkt, a["Wkt1"].rearrange("(k p) n -> p k n", k=8), "ld_w1")
            load(wv1raw, a["Wv1"].rearrange("(k p) n -> p k n", k=2), "ld_wv1")
            sp.wait_ge(S["y"], 3)
            load(wo1, a["Wo1"].rearrange("(k p) n -> p k n", k=8), "ld_wo1")
            load(aw, a["A1"].rearrange("(w k p) n -> p w k n", w=4, k=2), "ld_aw")

            sp.wait_ge(S["skips"], 1)
            sp.wait_ge(S["m1_start"], 1)

            def kept(eng, s):
                f = eng.value_load(sup[0:1, 0, bass.ds(s, 1)], min_val=0, max_val=1)
                n = eng.value_load(sup[0:1, 1, bass.ds(s, 1)], min_val=0, max_val=NSUP)
                return f, n

            with sp.Fori(0, NSUP) as s:
                f, n = kept(sp, s)
                with sp.If(f > 0):
                    for b in range(2):
                        sp.wait_ge(S["m1_split"], 2 * n + b + 1)
                        load(raw[:, 0, :], ctx_t[0:P, bass.ds((2 * s + b) * CH, CH)], "m1_raw")
                        load(raw[0:64, 1, :], ctx_t[P:CKV, bass.ds((2 * s + b) * CH, CH)], "m1_raw")
                        sp.wait_ge(S["m1_negm"], 2 * n + b + 1)
                        load(mq4[:, b * CH // 4:(b + 1) * CH // 4], a["mask_q"][:, bass.ds((2 * s + b) * (CH // 4), CH // 4)], f"m1_mask{b}")

            sp.wait_ge(S["m1_end"], 1)
            with sp.Fori(0, NSUP) as s:
                f, n = kept(sp, s)
                with sp.If(f > 0):
                    for b in range(2):
                        c = 2 * s + b
                        sp.wait_ge(S["e1_split"], 2 * n + b + 1)
                        load(raw[:, 0, :], ctx_t[0:P, bass.ds(c * CH, CH)], "e1_raw")
                        load(raw[0:64, 1, :], ctx_t[P:CKV, bass.ds(c * CH, CH)], "e1_raw")
                        load(raw[64:P, 1, :], ctx_t[P:CKV, bass.ds(c * CH, CH)], "e1_raw")
                        sp.wait_ge(S["e1_masked"], HALVES * (2 * n + b) + HALVES)
                        carry_wait()
                        load(mk4.rearrange("p (b t q) -> p b t q", b=2, t=TPC)[:, b, :, :], a["mask_k"][bass.ds(c * CH, CH), :]
                             .rearrange("(t p) q -> p t q", p=P), f"e1_mask{b}")

            sp.wait_ge(S["x_done"], 1)
            sp.dma_start(out, x[:, :]).then_inc(S["stored"], 16)
            sp.wait_ge(S["stored"], 16)

        @block.gpsimd
        def _(pool):
            pool.sem_inc(S["m0_kabs"], 2)
            pool.sem_inc(S["e0_lo"], 1)
            pool.sem_inc(S["m1_negm"], 2)
            pool.sem_inc(S["e1_split"], 1)
            def carry_waits():
                nc.gpsimd.tensor_tensor(pause[:, 2:3], pause[:, 1:2], pause[:, 1:2], ALU.add)

            powers = [0]

            def power(x, exponent):
                powers[0] += 1
                pool.wait_ge(S["to_power"], powers[0])
                nc.gpsimd.tensor_tensor(x, x, exponent, ALU.pow).then_inc(S["power"], 1)

            nc.gpsimd.memset(wqp, 0.0).then_inc(S["wqp_zero"], 1)
            nc.gpsimd.memset(wqp_b, 0.0).then_inc(S["wqp_zero"], 1)
            nc.gpsimd.memset(kabs, 0.0).then_inc(S["kabs_zero"], 1)
            pool.wait_ge(S["wqp_zero"], 2)
            pool.wait_ge(S["kabs_zero"], 1)
            nc.gpsimd.memset(ks[96:P, HQ + 4 * CH:].bitcast(F32), 1.0).then_inc(S["ks_ones"], 1)
            pool.wait_ge(S["ks_ones"], 1)
            nc.gpsimd.memset(expo[:, 0:1], -0.5).then_inc(S["expo"], 1)
            nc.gpsimd.memset(expo[:, 1:3], 0.5).then_inc(S["expo"], 1)
            nc.gpsimd.memset(pause[:, 1:2], 0.0).then_inc(S["expo"], 1)
            pool.wait_ge(S["expo"], 3)
            power(rstd[:, :], expo[:, 0:1])
            pool.wait_ge(S["wqp_zero"], 2)
            pool.wait_ge(S["ld_wq0"], 32)
            for e in range(2):
                for slot in range(3):
                    for k in range(2):
                        nc.gpsimd.tensor_copy(
                            lo_rows(wqp[:, k, :])[:, :, e, slot, e, :],
                            wq0[:, k, :].rearrange("p (g e d) -> p g e d", g=GROUPS, e=2)[:, :, e, :])
                    last = nc.gpsimd.tensor_copy(
                        lo_rows(wqp_b)[:, :, e, slot, e, :],
                        wq0[0:1, 2, :].rearrange("p (g e d) -> p g e d", g=GROUPS, e=2)[:, :, e, :])
            last.then_inc(S["wqp"], 1)

            pool.wait_ge(S["kabs_zero"], 1)
            pool.wait_ge(S["qs_ps"], 1)

            def key_maxima(c, b):
                pool.wait_ge(S["m0_keys"], 4 * c + 8)
                pool.wait_ge(S["m0_kabs"], c + 2)
                nc.gpsimd.tensor_tensor(ksq, kn[:, b, :, :].bitcast(F32), kn[:, b, :, :].bitcast(F32),
                                        ALU.mult).then_inc(S["m0_ksq"], 1)
                pool.wait_ge(S["m0_ksq"], c + 1)
                nc.gpsimd.tensor_tensor(kabs, kabs, ksq, ALU.add).then_inc(S["m0_kabs"], 1)

            with pool.Fori(0, NCH, 2) as c:
                for b in range(2):
                    key_maxima(c + b, b)

            power(kmax[:, :], expo[:, 1:3])
            pool.wait_ge(S["m0_red"], H * NCH + 2)
            pool.wait_ge(S["m0_kabs"], NCH + 2)
            pool.wait_ge(S["power"], 2)
            nc.gpsimd.memset(ks[96:P, 0:HQ + 4 * CH].bitcast(F32), 1.0).then_inc(S["ks_ones"], 1)
            pool.wait_ge(S["ks_ones"], 2)

            def split_lo0(c, b):
                pool.wait_ge(S["e0_raw"], 48 * (c + 1))
                pool.wait_ge(S["e0_hi"], c + 2)
                pool.wait_ge(S["e0_lo"], c + 1)
                carry_waits()
                nc.gpsimd.tensor_copy(hi_tmp[:, :], raw[:, 1, :]).then_inc(S["hi_tmp"], 1)
                nc.gpsimd.tensor_tensor(ct[:, b, X_AL, :], raw[:, 0, :], ct[:, b, X_AH, :].bitcast(F32),
                                        ALU.subtract).then_inc(S["e0_alo"], 1)
                pool.wait_ge(S["hi_tmp"], c + 1)
                pool.wait_ge(S["e0_alo"], c + 1)
                nc.gpsimd.tensor_tensor(ct[64:P, b, X_B, :], raw[64:P, 1, :], hi_tmp[64:P, :].bitcast(F32),
                                        ALU.subtract).then_inc(S["e0_lo"], 1)

            with pool.Fori(0, NCH, 2) as c:
                for b in range(2):
                    split_lo0(c + b, b)

            power(rstd[:, :], expo[:, 0:1])
            pool.wait_ge(S["thr"], 1)
            pool.wait_ge(S["ld_ffw"], 32)
            pool.wait_ge(S["o0_read"], 1)
            for k, w in ((0, ffw[:, 0:2048]), (1, ffw[:, 2048:4096])):
                nc.gpsimd.tensor_scalar(nm[:, :], w, thr[:, 2 + k:3 + k], None, ALU.is_lt).then_inc(S["tern"], 1)
                pool.wait_ge(S["tern"], 3 * k + 1)
                nc.gpsimd.tensor_scalar(w, w, thr[:, k:k + 1], None, ALU.is_gt).then_inc(S["tern"], 1)
                pool.wait_ge(S["tern"], 3 * k + 2)
                nc.gpsimd.tensor_tensor(w, w, nm[:, :], ALU.subtract).then_inc(S["tern"], 1)
                pool.wait_ge(S["tern"], 3 * k + 3)

            power(rstd[:, :], expo[:, 0:1])
            power(rstd[:, :], expo[:, 0:1])
            power(rstd[:, :], expo[:, 0:1])
            pool.wait_ge(S["power"], 6)
            nc.gpsimd.memset(x5[64:96, :, :].bitcast(F32), 1.0).then_inc(S["x5_ones"], 1)
            pool.wait_ge(S["x5_ones"], 1)
            nc.gpsimd.memset(nm[:, :], 0.0).then_inc(S["sums_zero"], 1)
            pool.wait_ge(S["skips"], 1)

            def kept(eng, s):
                f = eng.value_load(sup[0:1, 0, bass.ds(s, 1)], min_val=0, max_val=1)
                n = eng.value_load(sup[0:1, 1, bass.ds(s, 1)], min_val=0, max_val=NSUP)
                return f, n

            pool.wait_ge(S["m1_start"], 1)
            with pool.Fori(0, NSUP) as s:
                f, n = kept(pool, s)
                with pool.If(f > 0):
                    for b in range(2):
                        pool.wait_ge(S[f"m1_mask{b}"], 16 * n + 16)
                        pool.wait_ge(S["m1_red"], H * (2 * n + b) + H)
                        pool.wait_ge(S["m1_negm"], 2 * n + b + 2)
                        carry_waits()
                        nc.gpsimd.tensor_scalar(negm[:, b, :], mq[:, b, :], 1.0, BIG, ALU.subtract,
                                                ALU.mult).then_inc(S["m1_negm"], 1)
            pool.wait_ge(S["m1_end"], 1)
            with pool.Fori(0, NSUP) as s:
                f, n = kept(pool, s)
                with pool.If(f > 0):
                    for b in range(2):
                        g = 2 * n + b
                        pool.wait_ge(S["e1_raw"], 48 * (g + 1))
                        pool.wait_ge(S["e1_chunk"], g + 1)
                        pool.wait_ge(S["e1_split"], g + 1)
                        carry_waits()
                        nc.gpsimd.tensor_copy(ct[:, b, X_AH, :], raw[:, 0, :]).then_inc(S["e1_hi"], 1)
                        nc.gpsimd.tensor_copy(hi_tmp[:, :], raw[:, 1, :]).then_inc(S["e1_hi"], 1)
                        nc.gpsimd.tensor_copy(x5[0:64, b, :], raw[0:64, 1, :])
                        nc.gpsimd.tensor_copy(ct[0:64, b, X_B, :], raw[0:64, 1, :])
                        pool.wait_ge(S["e1_hi"], 3 * g + 2)
                        nc.gpsimd.tensor_tensor(ct[:, b, X_AL, :], raw[:, 0, :],
                                                ct[:, b, X_AH, :].bitcast(F32), ALU.subtract
                                                ).then_inc(S["e1_hi"], 1)
                        pool.wait_ge(S["e1_hi"], 3 * g + 3)
                        nc.gpsimd.tensor_tensor(ct[64:P, b, X_B, :], raw[64:P, 1, :],
                                                hi_tmp[64:P, :].bitcast(F32), ALU.subtract
                                                ).then_inc(S["e1_split"], 1)
            power(rstd[:, :], expo[:, 0:1])
            power(pr_flat[:, 0:HQ], slp[:, H:H + 1].to_broadcast([P, HQ]))
            power(rstd[:, :], expo[:, 0:1])

        @block.scalar
        def _(act):
            act.sem_inc(S["m0_keys"], 4)
            act.sem_inc(S["e0_hi"], 1)
            act.sem_inc(S["e0_exp"], 2)
            act.sem_inc(S["m1_split"], 1)
            act.sem_inc(S["e1_exp"], 2)
            act.sem_inc(S["e1_v"], 1)

            def transposed(tag, src, dst):
                act.wait_ge(S["turned"], turn(tag))
                nc.scalar.copy(dst, src).then_inc(S["turned_sb"], 1)

            def xnT_copy(tag):
                transposed(tag, ps[:, 0, 0:2 * T], xnT[:, :, :].rearrange("p k t -> p (k t)"))

            act.wait_ge(S["ld_wkv0"], 48)
            for w, i in ((wk0, 0), (wv0, 1)):
                nc.scalar.copy(w[:, W_AH, :], wraw[:, i, 0, :])
                last = nc.scalar.copy(w[:, W_BH, :], wraw[:, i, 1, :])
            last.then_inc(S["w0_hi"], 1)
            xnT_copy("x0")
            act.wait_ge(S["qs_ps"], 1)
            nc.scalar.mul(qs[0:96, :], bank(0, 4)[0:96, :], D0 ** -0.5).then_inc(S["qs_hi"], 1)

            def split_max0(c, b):
                act.wait_ge(S["m0_raw"], 32 * (c + 1))
                act.wait_ge(S["m0_proj"], 4 * c + 4)
                nc.scalar.copy(ct[:, b, X_AH, :], raw[:, 0, :])
                nc.scalar.copy(ct[0:64, b, X_B, :], raw[0:64, 1, :]).then_inc(S["m0_split"], 1)

            def keys_max0(c, b):
                act.wait_ge(S["m0_head"], H * c + H)
                act.wait_ge(S["m0_kabs"], c + 1)
                for i in range(4):
                    t, n = i // 2, i % 2
                    act.wait_ge(S["m0_proj"], 4 * c + i + 9)
                    nc.scalar.activation(kn[:, b, t, n * NB:(n + 1) * NB], ps[:, 4 + i, 0:NB], ACT.Identity,
                                         bias=bk0[:, t:t + 1]).then_inc(S["m0_keys"], 1)

            split_max0(0, 0)
            keys_max0(0, 0)
            act.wait_ge(S["ld_mask"], 16)
            act.wait_ge(S["qs_ps"], 1)
            for s in range(NSUP):
                nc.scalar.activation(ffw[:, 2048:2048 + 2 * CH], mflat[:, 2 * CH * s:2 * CH * (s + 1)],
                                     ACT.Copy, accum_out=cnt[:, s:s + 1]).then_inc(S["mask_sum"], 1)
                act.wait_ge(S["mask_sum"], s + 1)
            split_max0(1, 1)
            keys_max0(1, 1)
            act.wait_ge(S["ld_ffw"], 32)
            for k in range(2):
                nc.scalar.activation(pr_flat[:, 0:2048], ffw[:, 2048 * k:2048 * k + 2048], ACT.Abs,
                                     accum_out=wsum[:, k:k + 1]).then_inc(S["wsum"], 1)
                act.wait_ge(S["wsum"], k + 1)

            with act.Fori(2, NCH, 2) as c:
                for b in range(2):
                    split_max0(c + b, b)
                    keys_max0(c + b, b)

            act.wait_ge(S["m0_row"], 1)
            nc.scalar.copy(qs[96:P, :], bank(0, 4)[96:P, :]).then_inc(S["qs_max"], 1)

            def split_hi0(c, b):
                act.wait_ge(S["e0_raw"], 48 * (c + 1))
                act.wait_ge(S["e0_proj"], 11 * c + 11)
                nc.scalar.copy(ct[:, b, X_AH, :], raw[:, 0, :])
                nc.scalar.copy(ct[0:64, b, X_B, :], raw[0:64, 1, :]).then_inc(S["e0_hi"], 1)

            def key_block_hi(c, i, proj, stacked):
                t, n = i // 2, i % 2
                act.wait_ge(S["e0_proj"], proj)
                if stacked is not None and i == 0:
                    act.wait_ge(S[stacked[0]], stacked[1])
                nc.scalar.activation(khl[:, 0, t, n * NB:(n + 1) * NB], ps[:, 5 + i % 2, 0:NB], ACT.Identity,
                                     bias=bk0[:, t:t + 1]).then_inc(S["e0_khi"], 1)

            split_hi0(0, 0)
            for i in range(4):
                key_block_hi(0, i, 22 + i + 1, None)
            split_hi0(1, 1)
            act.wait_ge(S["nm_row"], 1)
            act.wait_ge(S["kmax"], 1)
            nc.scalar.copy(nm[:, :], bank(0, 4)).then_inc(S["nm"], 1)

            def chunk0(c, b, i2, keys, split):
                for u in range(HALVES):
                    g = HALVES * c + u
                    act.wait_ge(S["e0_ok"], g + 1)
                    act.wait_ge(S["e0_pv"], g + 11)
                    nc.scalar.activation(pr[:, (HALVES * b + u) % 4, :], bank(2 * (u % 2), 2), ACT.Exp
                                         ).then_inc(S["e0_exp"], 1)
                    if keys and u in (1, 3, 5, 7):
                        i = (u - 1) // 2
                        key_block_hi(c + 1, i, 22 + 11 * (c + 1) + K_ORDER[i], (f"e0_keys{b}", 192 * (i2 + 1)))
                    if split and u == 9:
                        split_hi0(c + 2, b)

            with act.Fori(0, (NCH - 2) // 2) as i2:
                for b in range(2):
                    chunk0(2 * i2 + b, b, i2, True, True)
            chunk0(NCH - 2, 0, NSUP - 1, True, False)
            chunk0(NCH - 1, 1, NSUP - 1, False, False)

            act.wait_ge(S["e0_pv"], HALVES * NCH + 14)
            nc.scalar.copy(oacc[:, :, :].rearrange("p a q -> p (a q)"), ps[:, 4, :]).then_inc(S["o0_read"], 1)

            def onT_copy(tag):
                transposed(tag, ps[:, 0, 0:2 * T], onT[:, :, :].rearrange("p k t -> p (k t)"))

            onT_copy("o0")

            xnT_copy("x1")
            act.wait_ge(S["ld_small"], 16 * 9)
            act.wait_ge(S["ga_proj"], 1)
            act.wait_ge(S["nbg"], 1)
            nc.scalar.activation(g1[:, 0:1], ps[:, 1, M0:M0 + 1], ACT.Exp, bias=nbg[:, 0:1], scale=-1.0
                                 ).then_inc(S["ga_exp"], 1)
            nc.scalar.copy(on[:, 0:M0], ps[:, 1, 0:M0])
            nc.scalar.copy(onT[0:M0, :, :].rearrange("p k t -> p (k t)"), ps[0:M0, 2, 0:2 * T]
                           ).then_inc(S["ga_kvq"], 1)
            act.wait_ge(S["ga_gate"], 1)
            nc.scalar.activation(g1[:, 2:3], g1[:, 1:2], ACT.Ln).then_inc(S["ga_log"], 1)
            act.wait_ge(S["ga_diff"], 1)
            nc.scalar.activation(xn[:, 0:T], xn[:, 0:T], ACT.Exp).then_inc(S["ga_decay"], 1)
            act.wait_ge(S["ga_reads"], 1)
            nc.scalar.copy(onT[0:M0, 0, :], ps[0:M0, 6, 0:T]).then_inc(S["ga_reads_sb"], 1)

            xnT_copy("x2")

            act.wait_ge(S["ld_wv1"], 16)
            nc.scalar.copy(wv1[:, W_AH, :], wv1raw[:, 0, :])
            nc.scalar.copy(wv1[:, W_BH, :], wv1raw[:, 1, :]).then_inc(S["wv1_hi"], 1)
            xnT_copy("x3")
            act.wait_ge(S["q1_ps"], 1)
            nc.scalar.mul(q1, bank(1, 2), D1 ** -0.5).then_inc(S["q1"], 1)
            act.wait_ge(S["qa_ps"], 1)
            nc.scalar.copy(asp[:, 0, :], bank(0, 4)).then_inc(S["qa_hi"], 1)
            act.wait_ge(S["qb_ps"], 1)
            nc.scalar.copy(asp[:, 2, :], bank(4, 4)).then_inc(S["qb_hi"], 1)

            act.wait_ge(S["skips"], 1)

            def kept(eng, s):
                f = eng.value_load(sup[0:1, 0, bass.ds(s, 1)], min_val=0, max_val=1)
                n = eng.value_load(sup[0:1, 1, bass.ds(s, 1)], min_val=0, max_val=NSUP)
                return f, n

            with act.Fori(0, NSUP) as s:
                f, n = kept(act, s)
                with act.If(f > 0):
                    for b in range(2):
                        g = 2 * n + b
                        act.wait_ge(S["m1_raw"], 32 * (g + 1))
                        act.wait_ge(S["m1_head"], H * g + H)
                        nc.scalar.copy(ct[:, b, X_AH, :], raw[:, 0, :])
                        nc.scalar.copy(ct[0:64, b, X_B, :], raw[0:64, 1, :]).then_inc(S["m1_split"], 1)

            act.wait_ge(S["m1_row"], 1)
            nc.scalar.copy(asp[64:96, 3, :], bank(0, 4)[64:96, :]).then_inc(S["a5_max"], 1)

            with act.Fori(0, NSUP) as s:
                f, n = kept(act, s)
                with act.If(f > 0):
                    for b in range(2):
                        g = 2 * n + b
                        for u in range(HALVES):
                            k = HALVES * g + u
                            act.wait_ge(S["e1_ok"], k + 1)
                            act.wait_ge(S["e1_pv"], k + 1)
                            act.wait_ge(S["e1_sum"], k + 1)
                            nc.scalar.activation(pr[:, (HALVES * b + u) % 4, :], bank(2 * (u % 2), 2), ACT.Exp
                                                 ).then_inc(S["e1_exp"], 1)
                            if u % 2 == 0:
                                act.wait_ge(S["e1_vps"], TPC * g + u // 2 + 1)
                                act.wait_ge(S["e1_pv"], k + 2)
                                nc.scalar.copy(v1[:, (TPC * b + u // 2) % 2, :], bank(6, 2)
                                               ).then_inc(S["e1_v"], 1)

            xnT_copy("x4")
            act.wait_ge(S["sa_proj"], 1)
            nc.scalar.copy(onT[:, :, :].rearrange("p k t -> p (k t)"), ps[:, 1, 0:2 * T])
            nc.scalar.copy(v17[:, 0:H * 17].rearrange("p (h d) -> p h d", h=H)[:, :, 0:D0],
                           ps[:, 2, 0:C].rearrange("p (h d) -> p h d", h=H)).then_inc(S["sa_kv"], 1)
            onT_copy("o4")
            xnT_copy("x5")


        @block.vector
        def _(dve):
            V = nc.vector
            steps = [0]

            def link(ins):
                steps[0] += 1
                ins.then_inc(S["dve_step"], 1)
                dve.wait_ge(S["dve_step"], steps[0])

            powers = [0]

            def on_pool(what):
                powers[0] += 1
                dve.sem_inc(S["to_power"], 1)
                dve.wait_ge(S["power"], powers[0])

            dve.sem_inc(S["m0_red"], 2)
            dve.sem_inc(S["m0_merge"], 1)
            dve.sem_inc(S["e0_v"], 1)
            dve.sem_inc(S["e0_klo"], 2)
            dve.sem_inc(S["m1_red"], 32)
            dve.sem_inc(S["m1_merge"], 1)
            dve.sem_inc(S["e1_masked"], 28)
            dve.sem_inc(S["e1_sum"], 4)

            def layernorm(tag):
                link(V.bn_stats(st6[:, :], x[:, :]))
                link(V.bn_aggr(mv[:, :], st6[:, :]))
                link(V.tensor_scalar(rstd[:, :], mv[:, 1:2], EPS_LN, None, ALU.add))
                on_pool("rstd")
                steps[0] += 1
                V.tensor_scalar(xn[:, :], x[:, :], mv[:, 0:1], rstd[:, 0:1], ALU.subtract, ALU.mult
                                ).then_inc(S["dve_step"], 1)
                dve.wait_ge(S["dve_step"], steps[0])

            def normed(tag):
                layernorm(tag)
                dve.sem_inc(S["to_turn"], 1)

            def add_to_x(src, row=None):
                if row is not None:
                    link(V.tensor_tensor(x[:, :], x[:, :], rows[:, row, :], ALU.add))
                link(V.tensor_tensor(x[:, :], x[:, :], src, ALU.add))

            dve.wait_ge(S["ld_x"], 16)
            normed("x0")
            V.memset(zero[:, :], 0.0).then_inc(S["zero"], 1)
            V.memset(mx[:, :], -3.0e38).then_inc(S["mx0"], 1)
            V.memset(ml[:, :, :], 0.0).then_inc(S["ml0"], 1)
            dve.wait_ge(S["ld_wkv0"], 48)
            dve.wait_ge(S["w0_hi"], 1)
            for w, i in ((wk0, 0), (wv0, 1)):
                V.tensor_tensor(w[:, W_AL, :], wraw[:, i, 0, :], w[:, W_AH, :].bitcast(F32), ALU.subtract)
                last = V.tensor_tensor(w[:, W_BL, :], wraw[:, i, 1, :], w[:, W_BH, :].bitcast(F32),
                                       ALU.subtract)
            last.then_inc(S["w0_lo"], 1)
            dve.wait_ge(S["ld_con"], 16)
            V.tensor_copy(selr[:, :], con[:, K_SEL:K_SEL + P]).then_inc(S["selr"], 1)
            dve.wait_ge(S["qs_ps"], 1)
            for t in range(2):
                link(V.tensor_scalar(xn[:, t * T:(t + 1) * T], ps[:, 4, t * T:(t + 1) * T], D0 ** -0.5, None,
                                     ALU.mult))
                link(V.tensor_reduce(qabs[:, t:t + 1], xn[:, t * T:(t + 1) * T], AX_X, ALU.max,
                                     apply_absolute_value=True))
                last = V.tensor_tensor(qn[:, 8 * t:8 * t + 8, :],
                                       xn[:, t * T:(t + 1) * T].unsqueeze(1).to_broadcast([P, 8, T]),
                                       con[:, K_HEAD:K_HEAD + 8].unsqueeze(2).to_broadcast([P, 8, T]),
                                       ALU.mult)
            last.then_inc(S["qn"], 1)
            dve.wait_ge(S["qs_hi"], 1)
            V.scalar_tensor_tensor(qs[32:64, :], bank(0, 4)[32:64, :], D0 ** -0.5, qs[32:64, :].bitcast(F32),
                                   ALU.mult, ALU.subtract).then_inc(S["qs_lo"], 1)

            dve.wait_ge(S["mx0"], 1)
            with dve.Fori(0, NCH) as c:
                dve.wait_ge(S["m0_merge"], c + 1)
                for h in range(H):
                    dve.wait_ge(S["m0_head"], H * c + h + 33)
                    V.tensor_reduce(cm[:, h:h + 1], ps[:, 2 * (h % 2):2 * (h % 2) + 2, 0:NB], AX_XY,
                                    ALU.max).then_inc(S["m0_red"], 1)
                dve.wait_ge(S["m0_red"], H * c + H + 2)
                V.tensor_tensor(mx[:, :], mx[:, :], cm[:, :], ALU.max).then_inc(S["m0_merge"], 1)
            dve.wait_ge(S["m0_merge"], NCH + 1)

            def minus_max(lo_name):
                link(V.tensor_scalar(mx[:, :], mx[:, :], -1.0, None, ALU.mult))
                link(V.tensor_copy(mhi[:, :], mx[:, :]))
                dve.wait_ge(S["ml0"], 1)
                link(V.tensor_copy(ml[:, :, 0], mhi[:, :].bitcast(F32)))
                link(V.tensor_tensor(ml[:, :, 1], mx[:, :], mhi[:, :].bitcast(F32), ALU.subtract))
                dve.sem_inc(S[lo_name], 1)

            link(V.tensor_scalar(mx[:, :], mx[:, :], CLAMP, -CLAMP, ALU.min, ALU.max))
            minus_max("m0_ml")
            dve.wait_ge(S["m0_kabs"], NCH + 2)
            for t in range(2):
                V.tensor_reduce(kmax[:, t:t + 1], kabs[:, t, :], AX_X, ALU.max).then_inc(S["kmaxs"], 1)
            dve.wait_ge(S["kmaxs"], 2)
            on_pool("kmax")
            link(V.tensor_tensor(bound[:, :], kmax[:, :], qabs[:, :], ALU.mult))
            dve.sem_inc(S["kmax"], 1)
            dve.wait_ge(S["bound_ps"], 1)
            link(V.tensor_reduce(bsum[:, :], ps[:, 5, 0:2], AX_X, ALU.max))
            link(V.tensor_scalar(bsum[:, :], bsum[:, :], 0.99 * CLAMP, None, ALU.is_lt))
            link(V.tensor_scalar(clipf[:, :], bsum[0:1, :], -1.0, 1.0, ALU.mult, ALU.add))
            dve.wait_ge(S["wsum_ps"], 1)
            link(V.tensor_scalar(thr[:, 0:2], ps[:, 6, 0:2], 1.0 / (FF * C), EPS_LN, ALU.mult, ALU.add))
            link(V.tensor_scalar(thr[:, 2:4], thr[:, 0:2], -0.5, None, ALU.mult))
            link(V.tensor_scalar(thr[:, 0:2], thr[:, 0:2], 0.5, None, ALU.mult))
            dve.sem_inc(S["thr"], 1)
            dve.wait_ge(S["mask_sum"], NSUP)
            V.memset(v17_v[:, :, :, :, D0], 1.0).then_inc(S["v_ones"], 1)
            clip = dve.value_load(clipf[0:1, 0:1], min_val=0, max_val=1)

            def key_block_lo(c, i):
                t, n = i // 2, i % 2
                dve.wait_ge(S["e0_khi"], 4 * c + i + 1)
                V.scalar_tensor_tensor(khl[:, 1, t, n * NB:(n + 1) * NB], ps[:, 5 + i % 2, 0:NB],
                                       bk0[:, t:t + 1], khl[:, 0, t, n * NB:(n + 1) * NB].bitcast(F32),
                                       ALU.add, ALU.subtract).then_inc(S["e0_klo"], 1)

            def value_tile(c, b, t, proj):
                dve.wait_ge(S["e0_proj"], proj)
                dve.wait_ge(S["e0_pv"], HALVES * c)
                V.tensor_copy(v17_v[:, b, t, :, 0:D0], ps[:, 7, 0:C].rearrange("p (h d) -> p h d", h=H)
                              ).then_inc(S["e0_v"], 1)

            dve.wait_ge(S["v_ones"], 1)
            for i in range(4):
                key_block_lo(0, i)
            for t in range(TPC):
                dve.wait_ge(S["e0_proj"], 22 + 4 + t + 1)
                V.tensor_copy(v17_v[:, 0, t, :, 0:D0], ps[:, 7, 0:C].rearrange("p (h d) -> p h d", h=H)
                              ).then_inc(S["e0_v"], 1)
            dve.wait_ge(S["nm"], 1)

            def chunk0(c, b, nxt):
                for u in range(HALVES):
                    k = HALVES * c + u
                    z = u % 2
                    s = bank(2 * z, 2)
                    with dve.If(clip > 0):
                        dve.wait_ge(S["e0_score"], k + 29)
                        V.scalar_tensor_tensor(s, nm[:, 1024 * z:1024 * z + 1024], CLAMP, s, ALU.add, ALU.min
                                               ).then_inc(S["clip_min"], 1)
                        dve.wait_ge(S["clip_min"], k + 1)
                        V.scalar_tensor_tensor(s, nm[:, 1024 * z:1024 * z + 1024], -CLAMP, s, ALU.add, ALU.max
                                               ).then_inc(S["clip_max"], 1)
                        dve.wait_ge(S["clip_max"], k + 1)
                        dve.sem_inc(S["e0_ok"], 1)
                    with dve.Else():
                        dve.wait_ge(S["e0_score"], k + 29)
                        dve.sem_inc(S["e0_ok"], 1)
                    if nxt:
                        if u in (1, 3, 5, 7):
                            key_block_lo(c + 1, (u - 1) // 2)
                        if u in VALUES_AT:
                            t = VALUES_AT.index(u)
                            value_tile(c + 1, 1 - b, t, 22 + 11 * (c + 1) + V_ORDER[t])

            with dve.Fori(0, NCH - 2, 2) as c:
                for b in range(2):
                    chunk0(c + b, b, True)
            chunk0(NCH - 2, 0, True)
            chunk0(NCH - 1, 1, False)

            dve.wait_ge(S["cnt_ps"], 1)
            link(V.tensor_scalar(cf[:, 0, 0:NSUP], ps[0:1, 5, 0:NSUP], 1.0, None, ALU.min))
            link(V.memset(cf[:, 1, :], 0.0))
            for s in range(1, NSUP + 1):
                link(V.tensor_tensor(cf[:, 1, s:s + 1], cf[:, 1, s - 1:s], cf[:, 0, s - 1:s], ALU.add))
            link(V.tensor_copy(sup[:, 0, 0:NSUP], cf[:, 0, 0:NSUP]))
            link(V.tensor_copy(sup[:, 1, :], cf[:, 1, :]))
            dve.sem_inc(S["skips"], 1)
            dve.wait_ge(S["ld_small"], 16 * 9)
            for s in range(4):
                link(V.tensor_scalar(enc[:, :, :], pk[:, :, :], 2 * s, 3, ALU.logical_shift_right,
                                     ALU.bitwise_and))
                link(V.tensor_scalar(wtf[:, :, 64 * s:64 * s + 64], enc[:, :, :], -1.0, fsc[:, 0:1], ALU.add,
                                     ALU.mult))
            link(V.tensor_scalar(neg[:, :], tri, 1.0, CLAMP, ALU.subtract, ALU.mult))
            link(V.tensor_scalar(nbg[:, :], nbg[:, :], -1.0, None, ALU.mult))
            dve.sem_inc(S["nbg"], 1)

            dve.wait_ge(S["o0_q"], 1)
            dve.wait_ge(S["ld_rows"], 16 * 7)
            o4 = ps[:, 1, :].rearrange("p (a j r) -> p a j r", a=4, j=4)
            on4 = on[:, :].rearrange("p (a j d) -> p a j d", a=4, j=4)
            rl4 = rl[:, :].rearrange("p (a j) -> p a j", a=4)
            link(V.reciprocal(rl4, o4[:, :, :, D0]))
            link(V.tensor_tensor(on4, o4[:, :, :, 0:D0], rl4.unsqueeze(3).to_broadcast([P, 4, 4, D0]), ALU.mult))
            link(V.tensor_tensor(on[:, :], on[:, :], rows[:, R_BV0, :], ALU.add))
            dve.sem_inc(S["to_turn"], 1)
            dve.wait_ge(S["y"], 1)
            add_to_x(ps[:, 3, 0:C], R_BO0)

            normed("x1")
            dve.wait_ge(S["ga_exp"], 1)
            link(V.tensor_scalar(g1[:, 0:1], g1[:, 0:1], 1.0, None, ALU.add))
            link(V.reciprocal(g1[:, 1:2], g1[:, 0:1]))
            link(V.tensor_scalar(g1[:, 1:2], g1[:, 1:2], 1e-8, None, ALU.add))
            dve.sem_inc(S["ga_gate"], 1)
            dve.wait_ge(S["ga_log"], 1)
            dve.wait_ge(S["turned_sb"], turn("x1"))
            link(V.tensor_scalar(xn[:, T:2 * T], ones, g1[:, 2:3], None, ALU.mult))
            dve.sem_inc(S["ga_lgb"], 1)
            dve.wait_ge(S["ga_cum"], 1)
            link(V.tensor_copy(g1[:, 3:4], ps[:, 4, T:T + 1]))
            link(V.tensor_scalar(xn[:, 0:T], ps[:, 4, 0:T], g1[:, 3:4], 0.0, ALU.subtract, ALU.min))
            dve.sem_inc(S["ga_diff"], 1)
            dve.wait_ge(S["ga_decay"], 1)
            dve.wait_ge(S["ga_scores"], 1)
            link(V.tensor_tensor(xn[:, 0:T], xn[:, 0:T], tri, ALU.mult))
            link(V.scalar_tensor_tensor(xn[:, 0:T], ps[:, 5, 0:T], (M0 * T) ** -0.5, xn[:, 0:T], ALU.mult,
                                        ALU.mult))
            dve.sem_inc(S["ga_w"], 1)
            dve.wait_ge(S["y"], 2)
            add_to_x(ps[:, 7, 0:C])

            normed("x2")
            dve.wait_ge(S["ff_h"], 1)
            hT = v17[:, 2048:2048 + FF].rearrange("p (k t) -> p k t", k=8)
            link(V.tensor_tensor(hT, bank(1, 2).rearrange("p (k t) -> p k t", k=8),
                                 b1c[:, :].unsqueeze(2).to_broadcast([P, 8, T]), ALU.add))
            link(V.tensor_scalar(hT, hT, 0.0, None, ALU.max))
            dve.sem_inc(S["ff_hsb"], 1)
            dve.wait_ge(S["y"], 3)
            add_to_x(ps[:, 3, 0:C], R_B2)

            layernorm("x3")
            link(V.bn_stats(st6[:, :], xn[:, :]))
            link(V.bn_aggr(mv[:, :], st6[:, :]))
            link(V.tensor_scalar(rstd[:, :], mv[:, 1:2], EPS_LN, None, ALU.add))
            on_pool("rstd")
            link(V.tensor_scalar(xn[:, :], xn[:, :], mv[:, 0:1], rstd[:, 0:1], ALU.subtract, ALU.mult))
            link(V.tensor_tensor(xn[:, :], xn[:, :], rows[:, R_GAM, :], ALU.mult))
            link(V.tensor_tensor(xn[:, :], xn[:, :], rows[:, R_BET, :], ALU.add))
            dve.sem_inc(S["to_turn"], 1)
            dve.wait_ge(S["wv1_hi"], 1)
            V.tensor_tensor(wv1[:, W_AL, :], wv1raw[:, 0, :], wv1[:, W_AH, :].bitcast(F32), ALU.subtract)
            V.tensor_tensor(wv1[:, W_BL, :], wv1raw[:, 1, :], wv1[:, W_BH, :].bitcast(F32), ALU.subtract
                            ).then_inc(S["wv1_lo"], 1)
            dve.wait_ge(S["qa_hi"], 1)
            V.tensor_tensor(asp[:, 1, :], bank(0, 4), asp[:, 0, :].bitcast(F32), ALU.subtract
                            ).then_inc(S["qa_lo"], 1)
            dve.wait_ge(S["qb_hi"], 1)
            V.tensor_tensor(asp[0:64, 3, :], bank(4, 4)[0:64, :], asp[0:64, 2, :].bitcast(F32), ALU.subtract
                            ).then_inc(S["qb_lo"], 1)
            link(V.memset(mx[:, :], -3.0e38))
            dve.sem_inc(S["m1_start"], 1)

            def kept(eng, s):
                f = eng.value_load(sup[0:1, 0, bass.ds(s, 1)], min_val=0, max_val=1)
                n = eng.value_load(sup[0:1, 1, bass.ds(s, 1)], min_val=0, max_val=NSUP)
                return f, n

            with dve.Fori(0, NSUP) as s:
                f, n = kept(dve, s)
                with dve.If(f > 0):
                    for b in range(2):
                        g = 2 * n + b
                        dve.wait_ge(S["m1_negm"], g + 3)
                        dve.wait_ge(S["m1_merge"], g + 1)
                        for h in range(H):
                            dve.wait_ge(S["m1_head"], H * g + h + 33)
                            dve.wait_ge(S["m1_red"], H * g + h + 32)
                            V.memset(pause[:, 0:1], 0.0)
                            nc.vector.tensor_tensor_reduce(
                                out=junk.rearrange("p (j n) -> p j n", j=2),
                                in0=ps[:, 2 * (h % 2):2 * (h % 2) + 2, 0:NB],
                                in1=negm[:, b, :].rearrange("p (j n) -> p j n", j=2),
                                scale=1.0, scalar=-3.0e38, op0=ALU.add, op1=ALU.max,
                                accum_out=cm[:, h:h + 1]).then_inc(S["m1_red"], 1)
                        dve.wait_ge(S["m1_red"], H * g + H + 32)
                        V.tensor_tensor(mx[:, :], mx[:, :], cm[:, :], ALU.max).then_inc(S["m1_merge"], 1)
            total = dve.value_load(sup[0:1, 1, NSUP:NSUP + 1], min_val=0, max_val=NSUP)
            dve.wait_ge(S["m1_merge"], 2 * total + 1)
            minus_max("m1_ml")
            dve.sem_inc(S["m1_end"], 1)

            def mask_and_sum(k, b, u):
                sl = pr[:, (HALVES * b + u) % 4, :].rearrange("p (h q) -> p h q", h=8)
                acc = nm[:, 1024 * (u % 2):1024 * (u % 2) + 1024]
                dve.wait_ge(S["e1_exp"], k + 3)
                V.tensor_tensor(sl, sl, mk[:, b, u // 2, :].unsqueeze(1).to_broadcast([P, 8, T]), ALU.mult
                                ).then_inc(S["e1_masked"], 1)
                dve.wait_ge(S["e1_masked"], k + 29)
                dve.wait_ge(S["e1_sum"], k + 4)
                V.tensor_tensor(acc, acc, pr[:, (HALVES * b + u) % 4, :], ALU.add).then_inc(S["e1_sum"], 1)

            dve.wait_ge(S["sums_zero"], 1)
            with dve.Fori(0, NSUP) as s:
                f, n = kept(dve, s)
                with dve.If(f > 0):
                    for b in range(2):
                        g = 2 * n + b
                        dve.wait_ge(S[f"e1_mask{b}"], 16 * n + 16)
                        for u in range(HALVES):
                            k = HALVES * g + u
                            dve.wait_ge(S["e1_score"], k + 3)
                            V.tensor_scalar(bank(2 * (u % 2), 2), bank(2 * (u % 2), 2), 80.0, None, ALU.min
                                            ).then_inc(S["e1_ok"], 1)
                            if u > 0:
                                mask_and_sum(k - 1, b, u - 1)
                        mask_and_sum(HALVES * g + HALVES - 1, b, HALVES - 1)
            total = dve.value_load(sup[0:1, 1, NSUP:NSUP + 1], min_val=0, max_val=NSUP)
            dve.wait_ge(S["e1_sum"], 2 * HALVES * total + 4)
            steps[0] += 1
            V.memset(st6[:, :], 0.0).then_inc(S["dve_step"], 1)
            dve.wait_ge(S["dve_step"], steps[0])
            dve.sem_inc(S["e1_sums"], 1)
            dve.wait_ge(S["o1_ps"], 1)
            link(V.reciprocal(pr[:, 0, :], bank(0, 2)))
            link(V.tensor_tensor(pr[:, 1, :], bank(4, 2), pr[:, 0, :], ALU.mult))
            dve.sem_inc(S["o1"], 1)
            dve.wait_ge(S["y"], 4)
            add_to_x(ps[:, 6, 0:C], R_BO1)

            sc = pr_flat[:, 0:HQ]
            sd = pr_flat[:, HQ:2 * HQ]
            sc3 = sc.rearrange("p (h q) -> p h q", h=H)
            sd3 = sd.rearrange("p (h q) -> p h q", h=H)
            over_heads = lambda m: m.unsqueeze(1).to_broadcast([P, H, T])
            normed("x4")
            link(V.memset(v17[:, 0:H * 17].rearrange("p (h d) -> p h d", h=H)[:, :, D0], 1.0))
            link(V.tensor_tensor(sd3, over_heads(dist), slp[:, 0:H].unsqueeze(2).to_broadcast([P, H, T]),
                                 ALU.mult))
            dve.wait_ge(S["sa_proj"], 1)
            for t in range(2):
                link(V.tensor_scalar(xn[:, t * T:(t + 1) * T], ps[:, 3, t * T:(t + 1) * T], 4.0, None, ALU.mult))
                link(V.tensor_tensor(nm[:, 1024 * t:1024 * t + 1024].rearrange("p (h q) -> p h q", h=8),
                                     xn[:, t * T:(t + 1) * T].unsqueeze(1).to_broadcast([P, 8, T]),
                                     con[:, K_HEAD:K_HEAD + 8].unsqueeze(2).to_broadcast([P, 8, T]), ALU.mult))
            dve.sem_inc(S["sa_q"], 1)
            dve.wait_ge(S["sa_scores"], 1)
            link(V.tensor_tensor(sc, bank(4, 4), sd, ALU.subtract))
            link(V.tensor_tensor(sc3, sc3, over_heads(tri), ALU.mult))
            link(V.tensor_tensor(sc3, sc3, over_heads(neg[:, :]), ALU.add))
            link(V.scalar_tensor_tensor(sd, sc, -1.0, sc, ALU.mult, ALU.max))
            link(V.tensor_scalar(sd, sd, 1.0, None, ALU.add))
            link(V.reciprocal(sd, sd))
            link(V.tensor_tensor(sc, sc, sd, ALU.mult))
            link(V.tensor_scalar(sc, sc, 1.0, 0.5, ALU.add, ALU.mult))
            on_pool("probs")
            dve.sem_inc(S["sa_p"], 1)
            dve.wait_ge(S["sa_pv"], 1)
            o17 = ps[:, 3, 0:H * 17].rearrange("p (h d) -> p h d", h=H)
            link(V.tensor_scalar(rl[:, :], o17[:, :, D0], 1e-6, None, ALU.add))
            link(V.reciprocal(rl[:, :], rl[:, :]))
            link(V.tensor_tensor(on[:, :].rearrange("p (h d) -> p h d", h=H), o17[:, :, 0:D0],
                                 rl[:, :].unsqueeze(2).to_broadcast([P, H, D0]), ALU.mult))
            dve.sem_inc(S["to_turn"], 1)
            dve.wait_ge(S["y"], 5)
            add_to_x(ps[:, 1, 0:C])

            magic = 12582912.0
            layernorm("x5")
            link(V.tensor_reduce(rstd[:, :], xn[:, :], AX_X, ALU.max, apply_absolute_value=True))
            link(V.tensor_scalar(rstd[:, :], rstd[:, :], 1e-5, None, ALU.max))
            link(V.reciprocal(rstd[:, :], rstd[:, :]))
            link(V.tensor_scalar(rstd[:, :], rstd[:, :], 127.0, None, ALU.mult))
            link(V.tensor_scalar(xn[:, :], xn[:, :], rstd[:, 0:1], None, ALU.mult))
            link(V.tensor_scalar(xn[:, :], xn[:, :], magic, magic, ALU.add, ALU.subtract))
            link(V.tensor_scalar(xn[:, :], xn[:, :], 127.0, -128.0, ALU.min, ALU.max))
            link(V.reciprocal(rstd[:, :], rstd[:, :]))
            link(V.tensor_scalar(xn[:, :], xn[:, :], rstd[:, 0:1], None, ALU.mult))
            dve.sem_inc(S["to_turn"], 1)
            dve.wait_ge(S["y"], 6)
            add_to_x(ps[:, 3, 0:C], R_FB)
            dve.sem_inc(S["x_done"], 1)

        @block.tensor
        def _(pe):
            mm = nc.tensor.matmul

            pe.sem_inc(S["m0_proj"], 8)
            pe.sem_inc(S["m0_head"], 32)
            pe.sem_inc(S["e0_proj"], 22)
            pe.sem_inc(S["e0_score"], 28)
            pe.sem_inc(S["e0_pv"], 14)
            pe.sem_inc(S["m1_head"], 32)
            pe.sem_inc(S["e1_score"], 2)
            pe.sem_inc(S["e1_pv"], 4)
            pe.sem_inc(S["e1_chunk"], 2)

            def transposes(tag, src, b=0):
                pe.wait_ge(S["to_turn"], turn(tag))
                for k in range(2):
                    last = nc.tensor.transpose(ps[:, b, k * T:(k + 1) * T], src[:, k * P:(k + 1) * P], ident)
                last.then_inc(S["turned"], 1)

            def from_xT(dst, xT, w, name):
                for k in range(2):
                    last = mm(dst, xT[:, k, :], w[:, k, :], start=(k == 0), stop=(k == 1))
                last.then_inc(S[name], 1)

            pe.wait_ge(S["ld_con"], 16)
            transposes("x0", xn)
            pe.wait_ge(S["turned_sb"], turn("x0"))
            pe.wait_ge(S["wqp"], 1)
            pe.wait_ge(S["ld_wq0"], 32)
            for h in range(H):
                dst = ps[:, h // 4, (h % 4) * T:(h % 4 + 1) * T]
                for k in range(2):
                    mm(dst, wqp[:, k, h * P:(h + 1) * P], xnT[:, k, :], start=(k == 0), stop=False)
                mm(dst, wqp_b[:, h * P:(h + 1) * P], ones[0:1, :], start=False, stop=True)
            for t in range(2):
                dst = ps[:, 4, t * T:(t + 1) * T]
                for k in range(2):
                    mm(dst, wq0[:, k, t * P:(t + 1) * P], xnT[:, k, :], start=(k == 0), stop=False)
                last = mm(dst, wq0[0:1, 2, t * P:(t + 1) * P], ones[0:1, :], start=False, stop=True)
            last.then_inc(S["qs_ps"], 1)

            def project_max0(c, b):
                pe.wait_ge(S["m0_split"], c + 1)
                for i in range(4):
                    t, n = i // 2, i % 2
                    pe.wait_ge(S["m0_keys"], 4 * c + i + 1)
                    dst = ps[:, 4 + i, 0:NB]
                    mm(dst, wk0[:, W_AH, t * P:(t + 1) * P], ct[:, b, X_AH, n * NB:(n + 1) * NB],
                       start=True, stop=False)
                    mm(dst, wk0[0:64, W_BH, t * P:(t + 1) * P], ct[0:64, b, X_B, n * NB:(n + 1) * NB],
                       start=False, stop=True).then_inc(S["m0_proj"], 1)

            def heads_max0(c, b, heads):
                for h in heads:
                    t = h // 8
                    if h % 8 == 0:
                        pe.wait_ge(S["m0_keys"], 4 * c + 2 * t + 6)
                    pe.wait_ge(S["m0_red"], H * c + h + 1)
                    for n in range(2):
                        last = mm(ps[:, 2 * (h % 2) + n, 0:NB], qn[:, h, :],
                                  kn[:, b, t, n * NB:(n + 1) * NB], start=True, stop=True)
                    last.then_inc(S["m0_head"], 1)

            pe.wait_ge(S["w0_hi"], 1)
            pe.wait_ge(S["qn"], 1)
            pe.wait_ge(S["qs_lo"], 1)
            project_max0(0, 0)
            with pe.Fori(0, NCH - 2, 2) as c:
                for b in range(2):
                    heads_max0(c + b, b, range(0, 4))
                    project_max0(c + b + 1, 1 - b)
                    heads_max0(c + b, b, range(4, H))
            heads_max0(NCH - 2, 0, range(0, 4))
            project_max0(NCH - 1, 1)
            heads_max0(NCH - 2, 0, range(4, H))
            heads_max0(NCH - 1, 1, range(H))

            def project0(c, b, i):
                t, n = i // 2, i % 2
                if i == 0:
                    pe.wait_ge(S["e0_lo"], c + 2)
                pe.wait_ge(S["e0_klo"], 4 * c + i + 1)
                dst = ps[:, 5 + i % 2, 0:NB]
                for j, (w, xx) in enumerate(PAIRS):
                    last = mm(dst, wk0[:, w, t * P:(t + 1) * P], ct[:, b, xx, n * NB:(n + 1) * NB],
                              start=(j == 0), stop=(j == 4))
                last.then_inc(S["e0_proj"], 1)

            def values0(c, b, t):
                pe.wait_ge(S["e0_v"], TPC * c + t + 1)
                for j, (w, xx) in enumerate(PAIRS):
                    last = mm(ps[:, 7, 0:C], ct[:, b, xx, t * P:(t + 1) * P], wv0[:, w, :],
                              start=(j == 0), stop=(j == 4))
                last.then_inc(S["e0_proj"], 1)

            def scores0(c, b, u):
                z, t = u % 2, u // 2
                pe.wait_ge(S["e0_exp"], HALVES * c + u + 1)
                for k in range(4):
                    gg = 4 * z + k
                    last = mm(ps[:, 2 * z + k // 2, (k % 2) * 256:(k % 2) * 256 + 256],
                              ks_v[:, b, gg, t * P:(t + 1) * P], qs[:, gg * 256:gg * 256 + 256],
                              start=True, stop=True)
                last.then_inc(S["e0_score"], 1)

            def weigh0(c, b, u):
                z, t = u % 2, u // 2
                pe.wait_ge(S["e0_exp"], HALVES * c + u + 3)
                pe.wait_ge(S["e0_v"], TPC * c + t + 2)
                for k in range(8):
                    h = 8 * z + k
                    j = h % 4
                    last = mm(ps[32 * j:32 * j + 17, 4, (h // 4) * T:(h // 4 + 1) * T],
                              v17_v[:, b, t, h, :], pr[:, (HALVES * b + u) % 4, k * T:(k + 1) * T],
                              start=False, stop=True, skip_group_check=True)
                last.then_inc(S["e0_pv"], 1)

            pe.wait_ge(S["w0_lo"], 1)
            pe.wait_ge(S["m0_ml"], 1)
            for h in range(H):
                last = mm(ps[96:P, h // 4, (h % 4) * T:(h % 4 + 1) * T], ml[:, h, :], ident,
                          start=True, stop=True)
            last.then_inc(S["m0_row"], 1)
            pe.wait_ge(S["m0_keys"], 4 * NCH + 4)
            pe.wait_ge(S["kmax"], 1)
            mm(ps[:, 5, 0:2], ones, bound[:, :], start=True, stop=True).then_inc(S["bound_ps"], 1)
            pe.wait_ge(S["wsum"], 2)
            mm(ps[:, 6, 0:2], ones, wsum[:, :], start=True, stop=True).then_inc(S["wsum_ps"], 1)
            pe.wait_ge(S["selr"], 1)
            pe.wait_ge(S["qs_max"], 1)
            for k in range(4):
                last = mm(ps[:, k, :], selr[:, :], qs[:, 512 * k:512 * k + 512], start=True, stop=True)
            last.then_inc(S["nm_row"], 1)
            pe.wait_ge(S["zero"], 1)
            mm(ps[:, 4, :], zero[:, 0:P], zero[:, :], start=True, stop=True)
            pe.wait_ge(S["thr"], 1)
            for i in range(4):
                project0(0, 0, i)
            for t in range(TPC):
                values0(0, 0, t)
            pe.wait_ge(S["nm"], 1)
            pe.wait_ge(S["ks_ones"], 2)
            pe.wait_ge(S["e0_keys0"], 192)
            scores0(0, 0, 0)

            def chunk0(c, b, i2, nxt):
                for u in range(HALVES):
                    if u + 1 < HALVES:
                        scores0(c, b, u + 1)
                    elif nxt:
                        pe.wait_ge(S[f"e0_keys{1 - b}"], 192 * (i2 + 1 + b))
                        scores0(c + 1, 1 - b, 0)
                    if nxt and u in KEYS_AT:
                        project0(c + 1, 1 - b, KEYS_AT.index(u))
                    if nxt and u in VALUES_AT:
                        values0(c + 1, 1 - b, VALUES_AT.index(u))
                    weigh0(c, b, u)

            with pe.Fori(0, (NCH - 2) // 2) as i2:
                for b in range(2):
                    chunk0(2 * i2 + b, b, i2, True)
            chunk0(NCH - 2, 0, NSUP - 1, True)
            chunk0(NCH - 1, 1, NSUP - 1, False)

            pe.wait_ge(S["mask_sum"], NSUP)
            pe.wait_ge(S["e0_klo"], 4 * NCH + 2)
            mm(ps[:, 5, 0:NSUP], ones, cnt[:, 0:NSUP], start=True, stop=True).then_inc(S["cnt_ps"], 1)
            pe.wait_ge(S["o0_read"], 1)
            for k in range(4):
                last = nc.tensor.transpose(ps[:, 1, k * T:(k + 1) * T], oacc[:, k, :], ident)
            last.then_inc(S["o0_q"], 1)
            transposes("o0", on)
            pe.wait_ge(S["turned_sb"], turn("o0"))
            pe.wait_ge(S["ld_small"], 16 * 9)
            from_xT(ps[:, 3, 0:C], onT, wo0, "y")

            transposes("x1", xn)
            pe.wait_ge(S["turned_sb"], turn("x1"))
            for k in range(2):
                mm(ps[:, 1, 0:M0 + 1], xnT[:, k, :], a0w[:, k, 0:M0 + 1], start=(k == 0), stop=(k == 1))
            for j in range(2):
                for k in range(2):
                    last = mm(ps[0:M0, 2, j * T:(j + 1) * T],
                              a0w[:, k, M0 + 1 + j * M0:M0 + 1 + (j + 1) * M0], xnT[:, k, :],
                              start=(k == 0), stop=(k == 1))
            last.then_inc(S["ga_proj"], 1)
            pe.wait_ge(S["ga_kvq"], 1)
            mm(ps[:, 5, 0:T], onT[0:M0, 0, :], onT[0:M0, 1, :], start=True, stop=True
               ).then_inc(S["ga_scores"], 1)
            pe.wait_ge(S["ga_lgb"], 1)
            mm(ps[:, 4, 0:T], xn[:, T:2 * T], tri, start=True, stop=True)
            mm(ps[:, 4, T:T + 1], tri, g1[:, 2:3], start=True, stop=True).then_inc(S["ga_cum"], 1)
            pe.wait_ge(S["ga_w"], 1)
            mm(ps[0:M0, 6, 0:T], on[:, 0:M0], xn[:, 0:T], start=True, stop=True).then_inc(S["ga_reads"], 1)
            pe.wait_ge(S["ga_reads_sb"], 1)
            mm(ps[:, 7, 0:C], onT[0:M0, 0, :], a0wo[:, :], start=True, stop=True).then_inc(S["y"], 1)

            transposes("x2", xn)
            pe.wait_ge(S["turned_sb"], turn("x2"))
            pe.wait_ge(S["tern"], 6)
            for n in range(8):
                for k in range(2):
                    last = mm(ps[:, 1 + n // 4, (n % 4) * T:(n % 4 + 1) * T], ffw1[:, k, n * P:(n + 1) * P],
                              xnT[:, k, :], start=(k == 0), stop=(k == 1))
            last.then_inc(S["ff_h"], 1)
            pe.wait_ge(S["ff_hsb"], 1)
            for n in range(8):
                last = mm(ps[:, 3, 0:C], v17[:, 2048 + n * T:2048 + (n + 1) * T], ffw2[:, n, :],
                          start=(n == 0), stop=(n == 7))
            last.then_inc(S["y"], 1)

            transposes("x3", xn)
            pe.wait_ge(S["turned_sb"], turn("x3"))
            pe.wait_ge(S["ld_w1"], 32)
            for n in range(8):
                for k in range(2):
                    last = mm(ps[:, 1 + n // 4, (n % 4) * T:(n % 4 + 1) * T], wq1[:, k, n * P:(n + 1) * P],
                              xnT[:, k, :], start=(k == 0), stop=(k == 1))
            last.then_inc(S["q1_ps"], 1)
            pe.wait_ge(S["q1"], 1)
            for e in range(2):
                for w, name in ((0, "qa_ps"), (1, "qb_ps")):
                    for h in range(e, H, 2):
                        last = mm(ps[:, 4 * w + h // 4, (h % 4) * T:(h % 4 + 1) * T],
                                  wkt[64 * e:64 * e + 64, h // 2, w * P:(w + 1) * P],
                                  q1[64 * e:64 * e + 64, (h // 2) * T:(h // 2 + 1) * T],
                                  start=True, stop=True)
                    if e == 1:
                        last.then_inc(S[name], 1)
                if e == 0:
                    last.then_inc(S["even_heads"], 1)
                    pe.wait_ge(S["even_heads"], 1)

            def kept(eng, s):
                f = eng.value_load(sup[0:1, 0, bass.ds(s, 1)], min_val=0, max_val=1)
                n = eng.value_load(sup[0:1, 1, bass.ds(s, 1)], min_val=0, max_val=NSUP)
                return f, n

            pe.wait_ge(S["qa_lo"], 1)
            pe.wait_ge(S["qb_lo"], 1)
            pe.wait_ge(S["skips"], 1)
            with pe.Fori(0, NSUP) as s:
                f, n = kept(pe, s)
                with pe.If(f > 0):
                    for b in range(2):
                        g = 2 * n + b
                        pe.wait_ge(S["m1_split"], g + 2)
                        for h in range(H):
                            pe.wait_ge(S["m1_red"], H * g + h + 31)
                            for j in range(2):
                                dst = ps[:, 2 * (h % 2) + j, 0:NB]
                                mm(dst, asp[:, 0, h * T:(h + 1) * T], ct[:, b, X_AH, j * NB:(j + 1) * NB],
                                   start=True, stop=False)
                                last = mm(dst, asp[0:64, 2, h * T:(h + 1) * T],
                                          ct[0:64, b, X_B, j * NB:(j + 1) * NB], start=False, stop=True)
                            last.then_inc(S["m1_head"], 1)

            pe.wait_ge(S["m1_ml"], 1)
            for h in range(H):
                last = mm(ps[64:96, h // 4, (h % 4) * T:(h % 4 + 1) * T], ml[:, h, :], ident,
                          start=True, stop=True)
            last.then_inc(S["m1_row"], 1)
            for k in (4, 5):
                mm(ps[:, k, :], zero[:, 0:P], zero[:, :], start=True, stop=True)

            def scores1(g, b, u):
                z, t = u % 2, u // 2
                pe.wait_ge(S["e1_exp"], HALVES * g + u + 1)
                passes = [(ct[:, b, X_AH], 0), (ct[:, b, X_AH], 1), (ct[:, b, X_AL], 0), (ct[:, b, X_B], 2)]
                for j in range(2):
                    cols = slice(1024 * z + 512 * j, 1024 * z + 512 * j + 512)
                    for i, (xx, w) in enumerate(passes):
                        mm(ps[:, 2 * z + j, :], xx[:, t * P:(t + 1) * P], asp[:, w, cols],
                           start=(i == 0), stop=False)
                    last = mm(ps[:, 2 * z + j, :], x5[0:96, b, t * P:(t + 1) * P], asp[0:96, 3, cols],
                              start=False, stop=True)
                last.then_inc(S["e1_score"], 1)

            def values1(g, b, t):
                pe.wait_ge(S["e1_v"], TPC * g + t + 1)
                for j in range(2):
                    for i, (w, xx) in enumerate(PAIRS):
                        last = mm(ps[:, 6 + j, :], ct[:, b, xx, t * P:(t + 1) * P],
                                  wv1[:, w, 512 * j:512 * j + 512], start=(i == 0), stop=(i == 4))
                last.then_inc(S["e1_vps"], 1)

            def weigh1(g, b, u):
                z, t = u % 2, u // 2
                pe.wait_ge(S["e1_masked"], HALVES * g + u + 29)
                pe.wait_ge(S["e1_v"], TPC * g + t + 2)
                for k in range(8):
                    h = 8 * z + k
                    e = 64 * (h % 2)
                    last = mm(ps[e:e + 64, 4 + z, ((h // 2) % 4) * T:((h // 2) % 4 + 1) * T],
                              v1[:, (TPC * b + t) % 2, h * D1:(h + 1) * D1],
                              pr[:, (HALVES * b + u) % 4, k * T:(k + 1) * T],
                              start=False, stop=True, skip_group_check=True)
                last.then_inc(S["e1_pv"], 1)
                return last

            pe.wait_ge(S["a5_max"], 1)
            pe.wait_ge(S["x5_ones"], 1)
            pe.wait_ge(S["wv1_lo"], 1)
            with pe.Fori(0, NSUP) as s:
                f, n = kept(pe, s)
                with pe.If(f > 0):
                    pe.wait_ge(S["e1_split"], 2 * n + 2)
                    scores1(2 * n, 0, 0)
                    values1(2 * n, 0, 0)
                    for i in range(2 * HALVES):
                        b, u = i // HALVES, i % HALVES
                        if i + 1 < 2 * HALVES:
                            b1, u1 = (i + 1) // HALVES, (i + 1) % HALVES
                            if u1 == 0:
                                pe.wait_ge(S["e1_split"], 2 * n + 3)
                            scores1(2 * n + b1, b1, u1)
                            if u1 % 2 == 0:
                                values1(2 * n + b1, b1, u1 // 2)
                        weigh1(2 * n + b, b, u)
                        if u == HALVES - 1:
                            pe.wait_ge(S["e1_pv"], HALVES * (2 * n + b) + HALVES + 4)
                            pe.sem_inc(S["e1_chunk"], 1)

            pe.wait_ge(S["e1_sums"], 1)
            for h in range(H):
                e, k = 64 * (h % 2), h // 2
                last = mm(ps[e:e + 64, k // 4, (k % 4) * T:(k % 4 + 1) * T], ones[:, 0:64],
                          nm[:, h * T:(h + 1) * T], start=True, stop=True)
            last.then_inc(S["o1_ps"], 1)
            pe.wait_ge(S["o1"], 1)
            pe.wait_ge(S["ld_wo1"], 16)
            for n in range(8):
                last = mm(ps[:, 6, 0:C], pr[:, 1, n * T:(n + 1) * T], wo1[:, n, :], start=(n == 0), stop=(n == 7))
            last.then_inc(S["y"], 1)

            transposes("x4", xn)
            pe.wait_ge(S["turned_sb"], turn("x4"))
            pe.wait_ge(S["ld_aw"], 16)
            for w, b in ((0, 3), (1, 1)):
                for t in range(2):
                    for k in range(2):
                        mm(ps[:, b, t * T:(t + 1) * T], aw[:, w, k, t * P:(t + 1) * P], xnT[:, k, :],
                           start=(k == 0), stop=(k == 1))
            from_xT(ps[:, 2, 0:C], xnT, aw[:, 2], "sa_proj")
            pe.wait_ge(S["sa_kv"], 1)
            pe.wait_ge(S["sa_q"], 1)
            for k in range(4):
                last = mm(ps[:, 4 + k, :], onT[:, k // 2, :], nm[:, 512 * k:512 * k + 512], start=True, stop=True)
            last.then_inc(S["sa_scores"], 1)
            pe.wait_ge(S["sa_p"], 1)
            for h in range(H):
                last = mm(ps[:, 3, h * 17:(h + 1) * 17], pr_flat[:, h * T:(h + 1) * T],
                          v17[:, h * 17:(h + 1) * 17], start=True, stop=True)
            last.then_inc(S["sa_pv"], 1)
            transposes("o4", on)
            pe.wait_ge(S["turned_sb"], turn("o4"))
            from_xT(ps[:, 1, 0:C], onT, aw[:, 3], "y")

            transposes("x5", xn)
            pe.wait_ge(S["turned_sb"], turn("x5"))
            from_xT(ps[:, 3, 0:C], xnT, wtf, "y")


def kernel(**inputs):
    import concourse.bacc as bacc
    from concourse.bass_utils import run_bass_kernel_spmd

    def at(name):
        return np.asarray(inputs[name])

    def row(v):
        return v.reshape(1, -1)

    def padded(w):
        return np.concatenate([w, w[P:CKV]], axis=0)

    mask = at("mask_1x1xSxS2_bk0")[0, 0]
    wkv1 = at("L1_xattn_Wkv")
    wk1t = wkv1[:, :INNER].T
    where = np.arange(P)
    feed = {
        "x": at("x")[0],
        "ctxT": at("ctx_768")[0].T,
        "mask_q": np.ascontiguousarray(mask).view(np.int32),
        "mask_k": np.ascontiguousarray(mask.T).view(np.int32),
        "Wq0": at("L0_xattn_Wq"), "bq0": row(at("L0_xattn_bq")),
        "Wk0": padded(at("L0_xattn_Wk")), "Wv0": padded(at("L0_xattn_Wv")),
        "bk0": at("L0_xattn_bk").reshape(2, P).T,
        "bv0": row(at("L0_xattn_bv")), "bo0": row(at("L0_xattn_bo")), "b2": row(at("L0_ffn_b2")),
        "gamma": row(at("L1_xattn_ln_gamma")), "beta": row(at("L1_xattn_ln_beta")),
        "bo1": row(at("L1_xattn_bo")), "fbias": row(at("L1_ffn_bias")),
        "Wo0": at("L0_xattn_Wo"),
        "A0": np.concatenate([at("L0_attn_Wk").T, at("L0_attn_Wg").T, at("L0_attn_Wv").T,
                              at("L0_attn_Wq").T], axis=1),
        "A0o": at("L0_attn_Wo").T, "bg": row(at("L0_attn_bg")),
        "b1": at("L0_ffn_b1").reshape(FF // P, P).T,
        "W1T": at("L0_ffn_W1").T, "W2T": at("L0_ffn_W2").T,
        "slopes": row(at("L1_attn_alibi_slopes")), "power": row(at("L1_attn_power")),
        "fscale": row(at("L1_ffn_weight_scale")),
        "packed": at("L1_ffn_packed_weight").reshape(64, C).T,
        "Wq1": at("L1_xattn_Wq"),
        "Wkt1": np.concatenate([wk1t, wk1t[:, P:CKV]], axis=1),
        "Wv1": padded(wkv1[:, INNER:]),
        "Wo1": at("L1_xattn_Wo"),
        "A1": np.concatenate([at("L1_attn_Wq").T, at("L1_attn_Wk").T, at("L1_attn_Wv").T,
                              at("L1_attn_Wo").T], axis=0),
        "constants": np.concatenate([
            where[:, None] == where[None, :], where[:, None] <= where[None, :], np.ones((P, P)),
            np.abs(where[:, None] - where[None, :]), np.repeat(where[:, None] >= 96, P, axis=1),
            where[:, None] // D0 == np.arange(8)[None, :]], axis=1).astype(np.float32),
    }
    feed = {k: np.ascontiguousarray(v) for k, v in feed.items()}
    nc = bacc.Bacc("TRN2", target_bir_lowering=False, num_devices=1)
    a = {k: nc.dram_tensor("in_" + k, v.shape, mybir.dt.from_np(v.dtype), kind="ExternalInput").ap()
         for k, v in feed.items()}
    out = nc.dram_tensor("out", (1, T, C), F32, kind="ExternalOutput").ap()
    perceiver(nc, a, out[0])
    r = run_bass_kernel_spmd(nc, [{"in_" + k: v for k, v in feed.items()}], core_ids=[0])
    return r.results[0]["out"]
```

```python
from contextlib import ExitStack

import numpy as np

import concourse.bass as bass
from concourse import mybir

F32 = mybir.dt.float32
F32R = mybir.dt.float32r
BF16 = mybir.dt.bfloat16
I32 = mybir.dt.int32
U8 = mybir.dt.uint8
ALU = mybir.AluOpType
ACT = mybir.ActivationFunctionType
AX_X = mybir.AxisListType.X
AX_XY = mybir.AxisListType.XY

P = 128
T = 128
C = 256
CKV = 192
S2 = 12544
H = 16
HQ = H * T
D0 = C // H
D1 = 64
INNER = H * D1
M0 = 64
FF = 4 * C
CH = 896
NCH = S2 // CH
TPC = CH // P
NB = CH // 2
HALVES = 2 * TPC
GROUPS = H // 2
NSUP = NCH // 2
WARM_UP = 14
CLAMP = 10000.0
EPS_LN = 1e-5
BIG = 1.0e30

K_ID, K_TRI, K_ONE, K_DIST, K_SEL, K_HEAD = 0, 128, 256, 384, 512, 640
K_PAR = 648
K_END = 650

R_BV0, R_BO0, R_B2, R_GAM, R_BET, R_BO1, R_FB = range(7)

W_AH, W_AL, W_BH, W_BL = range(4)
X_AH, X_AL, X_B = range(3)
PAIRS = [(W_AH, X_AH), (W_AL, X_AH), (W_AH, X_AL), (W_BH, X_B), (W_BL, X_B)]

KEYS_AT = [0, 1, 2, 3]
VALUES_AT = [4, 5, 6, 7, 8, 9, 10]
K_ORDER = [1 + sorted(KEYS_AT + VALUES_AT).index(u) for u in KEYS_AT]
V_ORDER = [1 + sorted(KEYS_AT + VALUES_AT).index(u) for u in VALUES_AT]


TURNS = ["x0", "o0", "x1", "x2", "x3", "x4", "o4", "x5"]


HEAD_BANKS = (0, 2, 6)


def head_bank(b, h):
    return HEAD_BANKS[(h + b) % 3]


def last_user(b, h):
    at, c = head_bank(b, h), 0
    while True:
        h -= 1
        if h < 0:
            h, b, c = H - 1, 1 - b, c - 1
        if head_bank(b, h) == at:
            return c, h


def turn(tag):
    return TURNS.index(tag) + 1


class Signals(dict):

    def __init__(self, nc, ctx):
        super().__init__()
        self.nc, self.ctx = nc, ctx

    def __missing__(self, name):
        self[name] = self.ctx.enter_context(self.nc.semaphore(name))
        return self[name]


def perceiver(nc, a, out):
    with ExitStack() as ctx:
        S = Signals(nc, ctx)

        def sb(name, shape, dt=F32):
            return ctx.enter_context(nc.sbuf_tensor(name, shape, dt))

        ps = ctx.enter_context(nc.psum_tensor("ps", [P, 8, 512], F32))

        raw = sb("raw", [P, 2, CH])
        ct = sb("ct", [P, 2, 3, CH], F32R)
        khl = sb("khl", [P, 2, 2, CH], F32R)
        ks = sb("ks", [P, 2 * GROUPS * CH], F32R)
        ks_v = ks[:, :].rearrange("p (b g n) -> p b g n", b=2, g=GROUPS)
        qs = sb("qs", [P, HQ], F32R)
        nm = sb("nm", [P, HQ])
        v17 = sb("v17", [P, 2 * TPC * H * 17])
        v17_v = v17[:, :].rearrange("p (b t h d) -> p b t h d", b=2, t=TPC, h=H)
        pr = sb("pr", [P, 4, 1024])
        pr_flat = pr[:, :, :].rearrange("p s n -> p (s n)")
        oacc = sb("oacc", [P, 4, T])
        oacc_flat = oacc[:, :, :].rearrange("p a q -> p (a q)")
        wk0 = sb("wk0", [P, 4, C], F32R)
        wv0 = sb("wv0", [P, 4, C], F32R)
        ffw = sb("ffw", [P, 4096])
        wraw = sb("wraw", [P, 2, 2, C])
        k0_at = 2 * GROUPS * CH - HQ - 4 * CH
        qn = ks[:, k0_at:k0_at + HQ].rearrange("p (h q) -> p h q", h=H)
        kn = ks[:, k0_at + HQ:].rearrange("p (b t n) -> p b t n", b=2, t=2)
        qp = ks[:, k0_at - 8 * T:k0_at].rearrange("p (l t e q) -> p l t e q", l=2, t=2, e=2)
        qp_raw = v17[:, 1024:1024 + 4 * T].rearrange("p (t e q) -> p t e q", t=2, e=2)
        asp = ks[:, 0:4 * HQ].rearrange("p (w n) -> p w n", w=4)
        wv1 = ks[:, 4 * HQ:4 * HQ + 4 * INNER].rearrange("p (w n) -> p w n", w=4)
        x5 = khl[:, 0, :, :]
        kabs = nm[:, 0:2 * CH].rearrange("p (t n) -> p t n", t=2)
        v17_half = TPC * H * 17
        ksq = v17[:, v17_half:v17_half + 2 * CH].rearrange("p (t n) -> p t n", t=2)
        scrap = v17[:, 0:1024].bitcast(BF16)
        acc = pr_flat[:, 0:4 * CH].bitcast(BF16).rearrange("p (j n) -> p j n", j=8)
        stage = [oacc_flat[:, 0:CH // 2].bitcast(BF16),
                 pr_flat[:, 4 * CH:4 * CH + CH // 2].bitcast(BF16)]
        con = sb("con", [P, K_END])
        rows = sb("rows", [P, 7, C])
        x = sb("x", [P, C])
        xn = sb("xn", [P, C])
        xnT = sb("xnT", [P, 2, T])
        wq0 = sb("wq0", [P, 3, C])
        bk0 = sb("bk0", [P, 2])
        wo0 = sb("wo0", [P, 2, C])
        zero = sb("zero", [P, 512], BF16)
        selr = sb("selr", [P, P], F32R)
        neg = sb("neg", [P, T])
        st6 = sb("st6", [P, 6])
        mv = sb("mv", [P, 2])
        rstd = sb("rstd", [P, 1])
        expo = sb("expo", [P, 3])
        cm = sb("cm", [P, H])
        mx = sb("mx", [P, H])
        mhi = sb("mhi", [P, H], F32R)
        ml = sb("ml", [P, H, 32])
        qabs = sb("qabs", [P, 2])
        kmax = sb("kmax", [P, 2])
        bound = sb("bound", [P, 2])
        bsum = sb("bsum", [P, 1])
        clipf = sb("clipf", [1, 1], I32)
        cnt = sb("cnt", [P, 8])
        cf = sb("cf", [1, 2, 8])
        cq = sb("cq", [1, 8, NSUP])
        sup = sb("sup", [1, 2, 8], I32)
        wsum = sb("wsum", [P, 2])
        thr = sb("thr", [P, 4])
        pause2 = sb("pause2", [P, 2])
        pause = sb("pause", [P, 4])
        rl = sb("rl", [P, H])
        on = sb("on", [P, C])
        onT = sb("onT", [P, 2, T])
        a0w = sb("a0w", [P, 2, 3 * M0 + 1])
        a0wo = sb("a0wo", [M0, C])
        nbg = sb("nbg", [P, 1])
        g1 = sb("g1", [P, 4])
        b1c = sb("b1c", [P, FF // P])
        slp = sb("slp", [P, H + 1])
        fsc = sb("fsc", [P, 1])
        pk = sb("pk", [P, 2, 64], I32)
        ffw1 = ffw[:, 0:2048].rearrange("p (k n) -> p k n", k=2)
        ffw2 = ffw[:, 2048:4096].rearrange("p (k n) -> p k n", k=8)
        wo1 = ffw[:, 0:2048].rearrange("p (k n) -> p k n", k=8)
        aw = ffw[:, 2048:4096].rearrange("p (w k n) -> p w k n", w=4, k=2)
        wq1 = pr_flat[:, 0:2048].rearrange("p (k n) -> p k n", k=2)
        wkt = pr_flat[:, 2048:4096].rearrange("p (k n) -> p k n", k=8)
        negm = khl[:, 1, :, :]
        junk = pr_flat[:, 0:2 * CH].rearrange("p (i j n) -> p i j n", i=2, j=2)
        wv1raw = v17[:, 0:2048].rearrange("p (k n) -> p k n", k=2)
        v1 = v17[:, 0:2048].rearrange("p (b n) -> p b n", b=2)
        q1 = v17[:, 2048:2048 + INNER]
        enc = wq0[:, 0, 0:2 * 64].bitcast(I32).rearrange("p (k n) -> p k n", k=2)
        wtf = wq0[:, 1:3, :]
        wraw_flat = wraw[:, :, :, :].rearrange("p i k n -> p (i k n)")
        mk4 = wraw[:, 0, :, :].rearrange("p k n -> p (k n)")[:, 0:2 * CH // 4].bitcast(I32)
        mq4 = wraw[:, 1, :, :].rearrange("p k n -> p (k n)")[:, 0:2 * CH // 4].bitcast(I32)
        mflat4 = ffw[:, 0:S2 // 4].bitcast(I32)
        mk = mk4.bitcast(U8).rearrange("p (b t q) -> p b t q", b=2, t=TPC)
        mq = mq4.bitcast(U8).rearrange("p (b n) -> p b n", b=2)
        mflat = mflat4.bitcast(U8)

        ident = con[:, K_ID:K_ID + P]
        tri = con[:, K_TRI:K_TRI + P]
        ones = con[:, K_ONE:K_ONE + P]
        dist = con[:, K_DIST:K_DIST + P]
        headsel = con[:, K_HEAD:K_HEAD + 8]

        def bank(b, n=1):
            return ps[:, b:b + n, :].rearrange("p b n -> p (b n)")

        ctx_t = a["ctxT"]

        block = ctx.enter_context(nc.Block())

        @block.sync
        def _(sp):
            def load(dst, src, name):
                sp.dma_start(dst, src).then_inc(S[name], 16)

            def carry_wait():
                sp.sem_inc(S["carried"], 1)

            load(x[:, :], a["x"], "ld_x")
            load(con[:, :], a["constants"], "ld_con")
            load(wq0[:, 0:2, :], a["Wq0"].rearrange("(k p) n -> p k n", k=2), "ld_wq0")
            load(wq0[0:1, 2, :], a["bq0"], "ld_wq0")
            load(wraw[:, 0, :, :], a["Wk0"].rearrange("(k p) n -> p k n", k=2), "ld_wkv0")
            load(wraw[:, 1, :, :], a["Wv0"].rearrange("(k p) n -> p k n", k=2), "ld_wkv0")
            load(bk0[:, :], a["bk0"], "ld_wkv0")

            def load_max0(c, first):
                if not first:
                    sp.wait_ge(S["m0_split"], c)
                load(raw[:, 0, :], ctx_t[0:P, bass.ds(c * CH, CH)], "m0_raw")
                load(raw[0:64, 1, :], ctx_t[P:CKV, bass.ds(c * CH, CH)], "m0_raw")

            load_max0(0, True)
            load(mflat4, a["mask_q"], "ld_mask")
            for r, name in ((R_BV0, "bv0"), (R_BO0, "bo0"), (R_B2, "b2"), (R_GAM, "gamma"),
                            (R_BET, "beta"), (R_BO1, "bo1"), (R_FB, "fbias")):
                load(rows[:, r, :], a[name].partition_broadcast(P).rearrange("p o n -> p (o n)"), "ld_rows")
            load(wo0[:, :, :], a["Wo0"].rearrange("(k p) n -> p k n", k=2), "ld_small")
            load(a0w[:, :, :], a["A0"].rearrange("(k p) n -> p k n", k=2), "ld_small")
            load(a0wo[:, :], a["A0o"], "ld_small")
            load(nbg[:, :], a["bg"].partition_broadcast(P).rearrange("p o n -> p (o n)"), "ld_small")
            load(b1c[:, :], a["b1"], "ld_small")
            load(slp[:, 0:H], a["slopes"].partition_broadcast(P).rearrange("p o n -> p (o n)"), "ld_small")
            load(slp[:, H:H + 1], a["power"].partition_broadcast(P).rearrange("p o n -> p (o n)"), "ld_small")
            load(fsc[:, :], a["fscale"].partition_broadcast(P).rearrange("p o n -> p (o n)"), "ld_small")
            load(pk[:, :, :], a["packed"].rearrange("(k p) n -> p k n", k=2), "ld_small")
            load_max0(1, False)
            sp.wait_ge(S["qp"], 1)
            qs_v = qs[:, :].rearrange("p (t g n) -> p t g n", t=2, g=4)
            for slot, part in ((0, 0), (1, 1), (2, 0)):
                for g in range(4):
                    sp.dma_start(qs_v[32 * slot:32 * slot + 32, :, g, :].bitcast(F32),
                                 qp[32 * g:32 * g + 32, part].rearrange("p t e q -> p t (e q)").bitcast(F32)
                                 ).then_inc(S["qs_rows"], 16)
            load_max0(2, False)
            load_max0(3, False)
            load_max0(4, False)
            load_max0(5, False)
            sp.wait_ge(S["mask_sum"], NSUP)
            load(ffw1, a["W1T"].rearrange("(k p) n -> p k n", k=2), "ld_ffw")
            load(ffw2, a["W2T"].rearrange("(k p) n -> p k n", k=8), "ld_ffw")

            with sp.Fori(6, NCH) as c:
                load_max0(c, False)

            def load_sum0(c):
                sp.wait_ge(S["e0_lo"], c + 1)
                load(raw[:, 0, :], ctx_t[0:P, bass.ds(c * CH, CH)], "e0_raw")
                load(raw[0:64, 1, :], ctx_t[P:CKV, bass.ds(c * CH, CH)], "e0_raw")
                load(raw[64:P, 1, :], ctx_t[P:CKV, bass.ds(c * CH, CH)], "e0_raw")

            def stack_keys(c, b):
                sp.wait_ge(S["e0_klo"], 4 * c + 6)
                carry_wait()
                sp.wait_ge(S["e0_score"], HALVES * (c + 1))
                for slot, part in ((0, 0), (1, 0), (2, 1)):
                    for g in range(4):
                        sp.dma_start(ks_v[32 * slot:32 * slot + 32, b, g::4, :].bitcast(F32),
                                     khl[32 * g:32 * g + 32, part, :, :].bitcast(F32)
                                     ).then_inc(S[f"e0_keys{b}"], 16)

            sp.wait_ge(S["m0_split"], NCH)
            load_sum0(0)
            with sp.Fori(0, NCH - 2, 2) as c:
                for b in range(2):
                    load_sum0(c + b + 1)
                    stack_keys(c + b, b)
            load_sum0(NCH - 1)
            stack_keys(NCH - 2, 0)
            stack_keys(NCH - 1, 1)

            sp.wait_ge(S["o0_read"], 1)
            load(wq1, a["Wq1"].rearrange("(k p) n -> p k n", k=2), "ld_w1")
            load(wkt, a["Wkt1"].rearrange("(k p) n -> p k n", k=8), "ld_w1")
            load(wv1raw, a["Wv1"].rearrange("(k p) n -> p k n", k=2), "ld_wv1")
            sp.wait_ge(S["y"], 3)
            load(wo1, a["Wo1"].rearrange("(k p) n -> p k n", k=8), "ld_wo1")
            load(aw, a["A1"].rearrange("(w k p) n -> p w k n", w=4, k=2), "ld_aw")

            sp.wait_ge(S["skips"], 1)

            total = sp.value_load(sup[0:1, 1, NSUP:NSUP + 1], min_val=0, max_val=NSUP)
            with sp.Fori(0, NSUP) as n:
                with sp.If(total - n > 0):
                    s = sp.value_load(sup[0:1, 0, bass.ds(n, 1)], min_val=0, max_val=NSUP - 1)
                    for b in range(2):
                        sp.wait_ge(S["m1_split"], 2 * n + b + 1)
                        load(raw[:, 0, :], ctx_t[0:P, bass.ds((2 * s + b) * CH, CH)], "m1_raw")
                        load(raw[0:64, 1, :], ctx_t[P:CKV, bass.ds((2 * s + b) * CH, CH)], "m1_raw")
                        sp.wait_ge(S["m1_negm"], 2 * n + b + 1)
                        load(mq4[:, b * CH // 4:(b + 1) * CH // 4], a["mask_q"][:, bass.ds((2 * s + b) * (CH // 4), CH // 4)], f"m1_mask{b}")

            sp.wait_ge(S["m1_split"], 2 * total + 1)
            carry_wait()
            with sp.Fori(0, NSUP) as n:
                with sp.If(total - n > 0):
                    s = sp.value_load(sup[0:1, 0, bass.ds(n, 1)], min_val=0, max_val=NSUP - 1)
                    for b in range(2):
                        c = 2 * s + b
                        sp.wait_ge(S["e1_split"], 2 * n + b + 1)
                        load(raw[:, 0, :], ctx_t[0:P, bass.ds(c * CH, CH)], "e1_raw")
                        load(raw[0:64, 1, :], ctx_t[P:CKV, bass.ds(c * CH, CH)], "e1_raw")
                        load(raw[64:P, 1, :], ctx_t[P:CKV, bass.ds(c * CH, CH)], "e1_raw")
                        sp.wait_ge(S["e1_masked"], HALVES * (2 * n + b) + HALVES)
                        carry_wait()
                        load(mk4.rearrange("p (b t q) -> p b t q", b=2, t=TPC)[:, b, :, :], a["mask_k"][bass.ds(c * CH, CH), :]
                             .rearrange("(t p) q -> p t q", p=P), f"e1_mask{b}")

            sp.wait_ge(S["x_done"], 1)
            sp.dma_start(out, x[:, :]).then_inc(S["stored"], 16)
            sp.wait_ge(S["stored"], 16)

        @block.gpsimd
        def _(pool):
            pool.sem_inc(S["m0_kabs"], 2)
            pool.sem_inc(S["e0_lo"], 1)
            pool.sem_inc(S["m1_negm"], 2)
            pool.sem_inc(S["e1_split"], 1)
            def carry_waits(at=2):
                nc.gpsimd.tensor_tensor(pause[:, at:at + 1], pause[:, 1:2], pause[:, 1:2], ALU.add)

            powers = [0]

            def power(x, exponent):
                powers[0] += 1
                pool.wait_ge(S["to_power"], powers[0])
                nc.gpsimd.tensor_tensor(x, x, exponent, ALU.pow).then_inc(S["power"], 1)

            nc.gpsimd.memset(expo[:, 0:1], -0.5).then_inc(S["expo"], 1)
            nc.gpsimd.memset(expo[:, 1:3], 0.5).then_inc(S["expo"], 1)
            nc.gpsimd.memset(pause[:, 1:2], 0.0).then_inc(S["expo"], 1)
            nc.gpsimd.memset(kabs, 0.0).then_inc(S["kabs_zero"], 1)
            nc.gpsimd.memset(acc, -3.0e38).then_inc(S["acc_init"], 1)
            pool.wait_ge(S["expo"], 3)
            power(rstd[:, :], expo[:, 0:1])
            pool.wait_ge(S["kabs_zero"], 1)
            pool.wait_ge(S["acc_init"], 1)
            pool.wait_ge(S["power"], 1)
            nc.gpsimd.memset(ks[96:P, 0:k0_at - 8 * T].bitcast(F32), 1.0).then_inc(S["ks_ones"], 1)
            pool.wait_ge(S["ks_ones"], 1)

            pool.wait_ge(S["kabs_zero"], 1)

            def key_maxima(c, b):
                pool.wait_ge(S["m0_keys"], 4 * c + 8)
                pool.wait_ge(S["m0_kabs"], c + 2)
                nc.gpsimd.tensor_tensor(ksq, kn[:, b, :, :].bitcast(F32), kn[:, b, :, :].bitcast(F32),
                                        ALU.mult).then_inc(S["m0_ksq"], 1)
                pool.wait_ge(S["m0_ksq"], c + 1)
                nc.gpsimd.tensor_tensor(kabs, kabs, ksq, ALU.add).then_inc(S["m0_kabs"], 1)

            def split_lo0(c, b):
                pool.wait_ge(S["e0_hi"], c + 1)
                pool.wait_ge(S["e0_lo"], c + 1)
                nc.gpsimd.tensor_tensor(ct[:, b, X_AL, :], raw[:, 0, :], ct[:, b, X_AH, :].bitcast(F32),
                                        ALU.subtract).then_inc(S["e0_alo"], 1)
                pool.wait_ge(S["e0_alo"], c + 1)
                nc.gpsimd.tensor_tensor(ct[64:P, b, X_B, :], raw[64:P, 1, :],
                                        ct[64:P, b, X_B, :].bitcast(F32), ALU.subtract
                                        ).then_inc(S["e0_lo"], 1)

            with pool.Fori(0, NCH - 2, 2) as c:
                for b in range(2):
                    key_maxima(c + b, b)
            key_maxima(NCH - 2, 0)
            pool.wait_ge(S["m0_kabs"], NCH + 1)
            split_lo0(0, 0)
            pool.wait_ge(S["e0_lo"], 2)
            key_maxima(NCH - 1, 1)
            split_lo0(1, 1)
            pool.wait_ge(S["e0_lo"], 3)
            power(kmax[:, :], expo[:, 1:3])
            pool.wait_ge(S["m0_ml"], 1)
            pool.wait_ge(S["m0_kabs"], NCH + 2)
            pool.wait_ge(S["power"], 2)
            nc.gpsimd.memset(ks[96:P, k0_at - 8 * T:].bitcast(F32), 1.0).then_inc(S["ks_ones"], 1)
            pool.wait_ge(S["ks_ones"], 2)
            with pool.Fori(2, NCH, 2) as c:
                for b in range(2):
                    split_lo0(c + b, b)

            pool.wait_ge(S["thr"], 1)
            pool.wait_ge(S["ld_ffw"], 32)
            pool.wait_ge(S["e0_lo"], NCH + 1)
            for n in range(4):
                w, k = ffw[:, 1024 * n:1024 * n + 1024], n // 2
                nc.gpsimd.tensor_scalar(wraw_flat, w, thr[:, 2 + k:3 + k], None, ALU.is_lt
                                        ).then_inc(S["tern"], 1)
                nc.gpsimd.tensor_scalar(w, w, thr[:, k:k + 1], None, ALU.is_gt).then_inc(S["tern"], 1)
                pool.wait_ge(S["tern"], 3 * n + 2)
                nc.gpsimd.tensor_tensor(w, w, wraw_flat, ALU.subtract).then_inc(S["tern"], 1)
                pool.wait_ge(S["tern"], 3 * n + 3)
            power(rstd[:, :], expo[:, 0:1])
            power(rstd[:, :], expo[:, 0:1])
            power(rstd[:, :], expo[:, 0:1])
            power(rstd[:, :], expo[:, 0:1])
            pool.wait_ge(S["power"], 6)
            nc.gpsimd.memset(x5[64:96, :, :].bitcast(F32), 1.0).then_inc(S["x5_ones"], 1)
            pool.wait_ge(S["x5_ones"], 1)
            nc.gpsimd.memset(nm[:, :], 0.0).then_inc(S["sums_zero"], 1)
            pool.wait_ge(S["skips"], 1)

            total = pool.value_load(sup[0:1, 1, NSUP:NSUP + 1], min_val=0, max_val=NSUP)
            with pool.Fori(0, NSUP) as n:
                with pool.If(total - n > 0):
                    for b in range(2):
                        pool.wait_ge(S[f"m1_mask{b}"], 16 * n + 16)
                        pool.wait_ge(S["m1_red"], H * (2 * n + b) + H)
                        pool.wait_ge(S["m1_negm"], 2 * n + b + 2)
                        carry_waits()
                        nc.gpsimd.tensor_scalar(negm[:, b, :], mq[:, b, :], 1.0, BIG, ALU.subtract,
                                                ALU.mult).then_inc(S["m1_negm"], 1)
            pool.wait_ge(S["m1_negm"], 2 * total + 2)
            carry_waits(3)
            with pool.Fori(0, NSUP) as n:
                with pool.If(total - n > 0):
                    for b in range(2):
                        g = 2 * n + b
                        pool.wait_ge(S["e1_raw"], 48 * (g + 1))
                        pool.wait_ge(S["m1_head"], 2 * H * total + 32 - H * (1 - b))
                        pool.wait_ge(S["e1_chunk"], g + 1)
                        pool.wait_ge(S["e1_split"], g + 1)
                        carry_waits()
                        zeros = lambda rows: pause[0:rows, 1:2].to_broadcast([rows, CH])
                        nc.gpsimd.tensor_tensor(ct[:, b, X_AH, :], raw[:, 0, :], zeros(P), ALU.add
                                                ).then_inc(S["e1_hi"], 1)
                        nc.gpsimd.tensor_tensor(ct[:, b, X_B, :], raw[:, 1, :], zeros(P), ALU.add
                                                ).then_inc(S["e1_hi"], 1)
                        nc.gpsimd.tensor_tensor(x5[0:64, b, :], raw[0:64, 1, :], zeros(64), ALU.add
                                                ).then_inc(S["e1_hi"], 1)
                        pool.wait_ge(S["e1_hi"], 4 * g + 3)
                        nc.gpsimd.tensor_tensor(ct[:, b, X_AL, :], raw[:, 0, :],
                                                ct[:, b, X_AH, :].bitcast(F32), ALU.subtract
                                                ).then_inc(S["e1_hi"], 1)
                        pool.wait_ge(S["e1_hi"], 4 * g + 4)
                        nc.gpsimd.tensor_tensor(ct[64:P, b, X_B, :], raw[64:P, 1, :],
                                                ct[64:P, b, X_B, :].bitcast(F32), ALU.subtract
                                                ).then_inc(S["e1_split"], 1)
            power(rstd[:, :], expo[:, 0:1])
            power(rstd[:, :], expo[:, 0:1])

        @block.scalar
        def _(act):
            act.sem_inc(S["m0_keys"], 4)
            act.sem_inc(S["m0_staged"], 8)
            act.sem_inc(S["e0_exp"], 2)
            act.sem_inc(S["m1_split"], 1)
            act.sem_inc(S["e1_exp"], 2)
            act.sem_inc(S["e1_v"], 1)

            def transposed(tag, src, dst):
                act.wait_ge(S["turned"], turn(tag))
                nc.scalar.copy(dst, src).then_inc(S["turned_sb"], 1)

            def xnT_copy(tag):
                transposed(tag, ps[:, 0, 0:2 * T], xnT[:, :, :].rearrange("p k t -> p (k t)"))

            act.wait_ge(S["ld_wkv0"], 48)
            for w, i in ((wk0, 0), (wv0, 1)):
                nc.scalar.copy(w[:, W_AH, :], wraw[:, i, 0, :])
                last = nc.scalar.copy(w[:, W_BH, :], wraw[:, i, 1, :])
            last.then_inc(S["w0_hi"], 1)
            xnT_copy("x0")

            def split_max0(c, b):
                act.wait_ge(S["m0_raw"], 32 * (c + 1))
                act.wait_ge(S["m0_proj"], 4 * c + 4)
                nc.scalar.copy(ct[:, b, X_AH, :], raw[:, 0, :])
                nc.scalar.copy(ct[0:64, b, X_B, :], raw[0:64, 1, :]).then_inc(S["m0_split"], 1)

            def key_block_max0(c, b, i):
                t, n = i // 2, i % 2
                if i == 0:
                    act.wait_ge(S["m0_head"], H * c + H)
                    act.wait_ge(S["m0_kabs"], c + 1)
                act.wait_ge(S["m0_proj"], 4 * c + i + 9)
                nc.scalar.activation(kn[:, b, t, n * NB:(n + 1) * NB], ps[:, 4 + i % 2, 0:NB], ACT.Identity,
                                     bias=bk0[:, t:t + 1]).then_inc(S["m0_keys"], 1)

            def split_hi0(c, b):
                act.wait_ge(S["e0_raw"], 48 * (c + 1))
                act.wait_ge(S["e0_proj"], 11 * c + 11)
                nc.scalar.copy(ct[:, b, X_AH, :], raw[:, 0, :])
                nc.scalar.copy(ct[:, b, X_B, :], raw[:, 1, :]).then_inc(S["e0_hi"], 1)

            def mask_sum(s):
                if s == 0:
                    act.wait_ge(S["ld_mask"], 16)
                    act.wait_ge(S["qp"], 1)
                else:
                    act.wait_ge(S["mask_sum"], s)
                nc.scalar.activation(scrap[:, 0:2 * CH], mflat[:, 2 * CH * s:2 * CH * (s + 1)],
                                     ACT.Copy, accum_out=cnt[:, s:s + 1]).then_inc(S["mask_sum"], 1)

            def chunk_max0(c, b, nxt=True, split=True, sums=()):
                for j in range(8):
                    at = head_bank(b, 2 * j + 1)
                    act.wait_ge(S["m0_head"], H * c + 2 * j + 34)
                    act.wait_ge(S["m0_acc"], 8 * c + j + 1)
                    nc.scalar.copy(stage[j % 2].rearrange("p (k n) -> p k n", k=2), ps[:, at:at + 2, 0:NB]
                                   ).then_inc(S["m0_staged"], 1)
                    if nxt and j in (1, 3, 4, 6):
                        key_block_max0(c + 1, 1 - b, (1, 3, 4, 6).index(j))
                    if split and j == 2:
                        split_max0(c + 2, b)
                    if j == 5:
                        for s in sums:
                            mask_sum(s)
                        if not split:
                            split_hi0(0, 0)

            split_max0(0, 0)
            for i in range(4):
                key_block_max0(0, 0, i)
            split_max0(1, 1)
            for c in range(4):
                chunk_max0(c, c % 2, sums=range(2 * c, min(2 * c + 2, NSUP)))
            with act.Fori(4, NCH - 2, 2) as c:
                for b in range(2):
                    chunk_max0(c + b, b)
            act.wait_ge(S["ld_ffw"], 32)
            act.wait_ge(S["mask_sum"], NSUP)
            for k in range(2):
                nc.scalar.activation(scrap, ffw[:, 2048 * k:2048 * k + 2048], ACT.Abs,
                                     accum_out=wsum[:, k:k + 1]).then_inc(S["wsum"], 1)
                act.wait_ge(S["wsum"], k + 1)
            act.wait_ge(S["m0_proj"], 4 * (NCH - 1) + 8)
            chunk_max0(NCH - 2, 0, split=False)

            def key_block_hi(c, i, proj, stacked):
                t, n = i // 2, i % 2
                act.wait_ge(S["e0_proj"], proj)
                if stacked is not None and i == 0:
                    act.wait_ge(S[stacked[0]], stacked[1])
                nc.scalar.activation(khl[:, 0, t, n * NB:(n + 1) * NB], ps[:, 5 + i % 2, 0:NB], ACT.Identity,
                                     bias=bk0[:, t:t + 1]).then_inc(S["e0_khi"], 1)

            for j in range(8):
                act.wait_ge(S["m0_head"], H * (NCH - 1) + 2 * j + 34)
                act.wait_ge(S["m0_acc"], 8 * (NCH - 1) + j + 1)
                nc.scalar.copy(stage[j % 2].rearrange("p (k n) -> p k n", k=2), ps[:, 2:4, 0:NB]
                               ).then_inc(S["m0_staged"], 1)
                if j < 4:
                    key_block_hi(0, j, 22 + j + 1, None)
            act.wait_ge(S["m0_proj"], 4 * NCH + 8)
            split_hi0(1, 1)
            act.wait_ge(S["m0_row"], 1)
            nc.scalar.copy(qs[96:P, :], bank(0, 4)[96:P, :]).then_inc(S["qs_max"], 1)
            act.wait_ge(S["kmaxs"], 2)
            for k in range(2):
                act.wait_ge(S["nm_row"], k + 1)
                nc.scalar.copy(nm[:, 1024 * k:1024 * k + 1024], bank(2 * k, 2)).then_inc(S["nm"], 1)

            def chunk0(c, b, i2, keys, split):
                for u in range(HALVES):
                    g = HALVES * c + u
                    act.wait_ge(S["e0_ok"], g + 1)
                    act.wait_ge(S["e0_pv"], g + 11)
                    nc.scalar.activation(pr[:, (HALVES * b + u) % 4, :], bank(2 * (u % 2), 2), ACT.Exp
                                         ).then_inc(S["e0_exp"], 1)
                    if keys and u - 1 in KEYS_AT:
                        i = KEYS_AT.index(u - 1)
                        key_block_hi(c + 1, i, 22 + 11 * (c + 1) + K_ORDER[i], (f"e0_keys{b}", 192 * (i2 + 1)))
                    if split and u == 9:
                        split_hi0(c + 2, b)

            with act.Fori(0, (NCH - 2) // 2) as i2:
                for b in range(2):
                    chunk0(2 * i2 + b, b, i2, True, True)
            chunk0(NCH - 2, 0, NSUP - 1, True, False)
            chunk0(NCH - 1, 1, NSUP - 1, False, False)

            act.wait_ge(S["e0_pv"], HALVES * NCH + 14)
            nc.scalar.copy(oacc[:, :, :].rearrange("p a q -> p (a q)"), ps[:, 4, :]).then_inc(S["o0_read"], 1)

            def onT_copy(tag):
                transposed(tag, ps[:, 0, 0:2 * T], onT[:, :, :].rearrange("p k t -> p (k t)"))

            onT_copy("o0")

            xnT_copy("x1")
            act.wait_ge(S["ld_small"], 16 * 9)
            act.wait_ge(S["ga_proj"], 1)
            act.wait_ge(S["nbg"], 1)
            nc.scalar.activation(g1[:, 0:1], ps[:, 1, M0:M0 + 1], ACT.Exp, bias=nbg[:, 0:1], scale=-1.0
                                 ).then_inc(S["ga_exp"], 1)
            nc.scalar.copy(on[:, 0:M0], ps[:, 1, 0:M0])
            nc.scalar.copy(onT[0:M0, :, :].rearrange("p k t -> p (k t)"), ps[0:M0, 2, 0:2 * T]
                           ).then_inc(S["ga_kvq"], 1)
            act.wait_ge(S["ga_gate"], 1)
            nc.scalar.activation(g1[:, 2:3], g1[:, 1:2], ACT.Ln).then_inc(S["ga_log"], 1)
            act.wait_ge(S["ga_diff"], 1)
            nc.scalar.activation(xn[:, 0:T], xn[:, 0:T], ACT.Exp).then_inc(S["ga_decay"], 1)
            act.wait_ge(S["ga_reads"], 1)
            nc.scalar.copy(onT[0:M0, 0, :], ps[0:M0, 6, 0:T]).then_inc(S["ga_reads_sb"], 1)

            xnT_copy("x2")

            act.wait_ge(S["ld_wv1"], 16)
            nc.scalar.copy(wv1[:, W_AH, :], wv1raw[:, 0, :])
            nc.scalar.copy(wv1[:, W_BH, :], wv1raw[:, 1, :]).then_inc(S["wv1_hi"], 1)
            xnT_copy("x3")
            for i in range(2):
                act.wait_ge(S["q1_ps"], i + 1)
                nc.scalar.mul(q1[:, 512 * i:512 * i + 512], ps[:, 1 + i, :], D1 ** -0.5).then_inc(S["q1"], 1)
            act.wait_ge(S["qa_ps"], 1)
            nc.scalar.copy(asp[:, 0, :], bank(0, 4)).then_inc(S["qa_hi"], 1)
            act.wait_ge(S["qb_ps"], 1)
            nc.scalar.copy(asp[:, 2, :], bank(4, 4)).then_inc(S["qb_hi"], 1)

            act.wait_ge(S["skips"], 1)

            total = act.value_load(sup[0:1, 1, NSUP:NSUP + 1], min_val=0, max_val=NSUP)
            with act.Fori(0, NSUP) as n:
                with act.If(total - n > 0):
                    for b in range(2):
                        g = 2 * n + b
                        act.wait_ge(S["m1_raw"], 32 * (g + 1))
                        act.wait_ge(S["m1_head"], H * g + H)
                        nc.scalar.copy(ct[:, b, X_AH, :], raw[:, 0, :])
                        nc.scalar.copy(ct[0:64, b, X_B, :], raw[0:64, 1, :]).then_inc(S["m1_split"], 1)

            act.wait_ge(S["m1_row"], 1)
            nc.scalar.copy(asp[64:96, 3, :], bank(0, 4)[64:96, :]).then_inc(S["a5_max"], 1)

            with act.Fori(0, NSUP) as n:
                with act.If(total - n > 0):
                    for b in range(2):
                        g = 2 * n + b
                        for u in range(HALVES):
                            k = HALVES * g + u
                            act.wait_ge(S["e1_ok"], k + 1)
                            act.wait_ge(S["e1_pv"], k + 1)
                            act.wait_ge(S["e1_sum"], k + 1)
                            nc.scalar.activation(pr[:, (HALVES * b + u) % 4, :], bank(2 * (u % 2), 2), ACT.Exp
                                                 ).then_inc(S["e1_exp"], 1)
                            if u % 2 == 0:
                                act.wait_ge(S["e1_vps"], TPC * g + u // 2 + 1)
                                act.wait_ge(S["e1_pv"], k + 2)
                                nc.scalar.copy(v1[:, (TPC * b + u // 2) % 2, :], bank(6, 2)
                                               ).then_inc(S["e1_v"], 1)

            xnT_copy("x4")
            act.wait_ge(S["sa_proj"], 1)
            nc.scalar.copy(onT[:, :, :].rearrange("p k t -> p (k t)"), ps[:, 1, 0:2 * T])
            nc.scalar.copy(v17[:, 0:H * 17].rearrange("p (h d) -> p h d", h=H)[:, :, 0:D0],
                           ps[:, 2, 0:C].rearrange("p (h d) -> p h d", h=H)).then_inc(S["sa_kv"], 1)
            for k in range(2):
                act.wait_ge(S["sa_soft"], k + 1)
                nc.scalar.activation(pr[:, k, :], pr[:, k, :], ACT.Ln, bias=expo[:, 1:2], scale=0.5
                                     ).then_inc(S["sa_ln"], 1)
            act.wait_ge(S["sa_ln"], 2)
            for k in range(2):
                nc.scalar.activation(pr[:, k, :], pr[:, k, :], ACT.Exp, scale=slp[:, H:H + 1]
                                     ).then_inc(S["sa_exp"], 1)
            onT_copy("o4")
            xnT_copy("x5")


        @block.vector
        def _(dve):
            V = nc.vector
            steps = [0]

            def link(ins):
                steps[0] += 1
                ins.then_inc(S["dve_step"], 1)
                dve.wait_ge(S["dve_step"], steps[0])

            powers = [0]

            def on_pool(what):
                powers[0] += 1
                dve.sem_inc(S["to_power"], 1)
                dve.wait_ge(S["power"], powers[0])

            dve.sem_inc(S["m0_red"], 8)
            dve.sem_inc(S["m0_acc"], 2)
            dve.sem_inc(S["m0_merge"], 2)
            dve.sem_inc(S["e0_v"], 1)
            dve.sem_inc(S["e0_klo"], 2)
            dve.sem_inc(S["m1_red"], 32)
            dve.sem_inc(S["m1_merge"], 1)
            dve.sem_inc(S["e1_masked"], 28)
            dve.sem_inc(S["e1_sum"], 4)

            def layernorm(tag):
                link(V.bn_stats(st6[:, :], x[:, :]))
                link(V.bn_aggr(mv[:, :], st6[:, :]))
                link(V.tensor_scalar(rstd[:, :], mv[:, 1:2], EPS_LN, None, ALU.add))
                on_pool("rstd")
                steps[0] += 1
                V.tensor_scalar(xn[:, :], x[:, :], mv[:, 0:1], rstd[:, 0:1], ALU.subtract, ALU.mult
                                ).then_inc(S["dve_step"], 1)
                dve.wait_ge(S["dve_step"], steps[0])

            def normed(tag):
                layernorm(tag)
                dve.sem_inc(S["to_turn"], 1)

            def add_to_x(src, row=None):
                if row is not None:
                    link(V.tensor_tensor(x[:, :], x[:, :], rows[:, row, :], ALU.add))
                link(V.tensor_tensor(x[:, :], x[:, :], src, ALU.add))

            dve.wait_ge(S["ld_x"], 16)
            normed("x0")
            V.memset(zero[:, :], 0.0).then_inc(S["zero"], 1)
            V.memset(mx[:, :], -3.0e38).then_inc(S["mx0"], 1)
            V.memset(ml[:, :, :], 0.0).then_inc(S["ml0"], 1)
            dve.wait_ge(S["ld_wkv0"], 48)
            dve.wait_ge(S["w0_hi"], 1)
            for w, i in ((wk0, 0), (wv0, 1)):
                V.tensor_tensor(w[:, W_AL, :], wraw[:, i, 0, :], w[:, W_AH, :].bitcast(F32), ALU.subtract)
                last = V.tensor_tensor(w[:, W_BL, :], wraw[:, i, 1, :], w[:, W_BH, :].bitcast(F32),
                                       ALU.subtract)
            last.then_inc(S["w0_lo"], 1)
            dve.wait_ge(S["ld_con"], 16)
            V.tensor_copy(selr[:, :], con[:, K_SEL:K_SEL + P]).then_inc(S["selr"], 1)
            dve.wait_ge(S["qs_ps"], 1)
            for t in range(2):
                qt = xn[:, t * T:(t + 1) * T]
                link(V.tensor_scalar(qt, ps[:, 4, t * T:(t + 1) * T], D0 ** -0.5, None, ALU.mult))
                last = V.tensor_tensor(qn[:, 8 * t:8 * t + 8, :], qt.unsqueeze(1).to_broadcast([P, 8, T]),
                                       con[:, K_HEAD:K_HEAD + 8].unsqueeze(2).to_broadcast([P, 8, T]),
                                       ALU.mult)
            last.then_inc(S["qn"], 1)
            for t in range(2):
                qt = xn[:, t * T:(t + 1) * T]
                link(V.tensor_reduce(qabs[:, t:t + 1], qt, AX_X, ALU.max, apply_absolute_value=True))
                link(V.tensor_tensor(qp_raw[:, t], qt.unsqueeze(1).to_broadcast([P, 2, T]),
                                     con[:, K_PAR:K_PAR + 2].unsqueeze(2).to_broadcast([P, 2, T]), ALU.mult))
            link(V.tensor_copy(qp[:, 0], qp_raw))
            link(V.tensor_tensor(qp[:, 1], qp_raw, qp[:, 0].bitcast(F32), ALU.subtract))
            dve.sem_inc(S["qp"], 1)

            dve.wait_ge(S["mx0"], 1)
            mx_e = mx[:, :].rearrange("p (j e) -> p j e", e=2)
            cm_e = cm[:, :].rearrange("p (j b) -> p j b", b=2)

            def reduce_head(c, b, h, bank=None):
                bank = head_bank(b, h) if bank is None else bank
                dve.wait_ge(S["m0_head"], H * c + h + 33)
                V.tensor_reduce(cm_e[:, h // 2:h // 2 + 1, b], ps[:, bank:bank + 2, 0:NB], AX_XY, ALU.max
                                ).then_inc(S["m0_red"], 1)

            def accumulate_head(c, j):
                dve.wait_ge(S["m0_staged"], 8 * c + j + 9)
                V.tensor_tensor(acc[:, j], acc[:, j], stage[j % 2], ALU.max).then_inc(S["m0_acc"], 1)

            def merge_max0(c, b):
                dve.wait_ge(S["m0_red"], 8 * c + 16)
                V.tensor_tensor(mx_e[:, :, 0], mx_e[:, :, 0], cm_e[:, :, b], ALU.max
                                ).then_inc(S["m0_merge"], 1)

            def chunk_max0(c, b, merge=True):
                dve.wait_ge(S["m0_merge"], c + 1)
                for j in range(8):
                    reduce_head(c, b, 2 * j)
                    if j == 1 and merge:
                        merge_max0(c - 1, 1 - b)
                    if j > 0:
                        accumulate_head(c, j - 1)
                accumulate_head(c, 7)

            dve.wait_ge(S["acc_init"], 1)
            chunk_max0(0, 0, merge=False)
            chunk_max0(1, 1)
            with dve.Fori(2, NCH - 2, 2) as c:
                for b in range(2):
                    chunk_max0(c + b, b)
            chunk_max0(NCH - 2, 0)

            def key_block_lo(c, i):
                t, n = i // 2, i % 2
                dve.wait_ge(S["e0_khi"], 4 * c + i + 1)
                V.scalar_tensor_tensor(khl[:, 1, t, n * NB:(n + 1) * NB], ps[:, 5 + i % 2, 0:NB],
                                       bk0[:, t:t + 1], khl[:, 0, t, n * NB:(n + 1) * NB].bitcast(F32),
                                       ALU.add, ALU.subtract).then_inc(S["e0_klo"], 1)

            dve.wait_ge(S["wsum"], 2)
            V.memset(v17_v[:, 0, :, :, D0], 1.0).then_inc(S["v_ones"], 1)
            dve.wait_ge(S["v_ones"], 1)
            dve.wait_ge(S["m0_merge"], NCH)
            for h in range(H):
                if h % 2 == 0:
                    reduce_head(NCH - 1, 1, h, 0)
                else:
                    accumulate_head(NCH - 1, h // 2)
                if h == 2:
                    merge_max0(NCH - 2, 0)
                if h in (2, 4, 6, 8):
                    key_block_lo(0, h // 2 - 1)
                if h >= H - TPC:
                    t = h - (H - TPC)
                    dve.wait_ge(S["e0_proj"], 22 + 4 + t + 1)
                    V.tensor_copy(v17_v[:, 0, t, :, 0:D0],
                                  ps[:, 7 if t % 2 == 0 else 4, 0:C].rearrange("p (h d) -> p h d", h=H)
                                  ).then_inc(S["e0_v"], 1)
            merge_max0(NCH - 1, 1)
            dve.wait_ge(S["m0_merge"], NCH + 2)
            dve.wait_ge(S["m0_acc"], 8 * NCH + 2)
            n = CH // 2
            while n >= CH // 8:
                link(V.tensor_tensor(acc[:, :, 0:n], acc[:, :, 0:n], acc[:, :, n:2 * n], ALU.max))
                n //= 2
            link(V.tensor_reduce(mx_e[:, :, 1], acc[:, :, 0:CH // 8], AX_X, ALU.max))

            def minus_max(lo_name):
                link(V.tensor_scalar(mx[:, :], mx[:, :], -1.0, None, ALU.mult))
                link(V.tensor_copy(mhi[:, :], mx[:, :]))
                dve.wait_ge(S["ml0"], 1)
                link(V.tensor_copy(ml[:, :, 0], mhi[:, :].bitcast(F32)))
                link(V.tensor_tensor(ml[:, :, 1], mx[:, :], mhi[:, :].bitcast(F32), ALU.subtract))
                dve.sem_inc(S[lo_name], 1)

            link(V.tensor_scalar(mx[:, :], mx[:, :], CLAMP, -CLAMP, ALU.min, ALU.max))
            minus_max("m0_ml")
            dve.wait_ge(S["m0_kabs"], NCH + 2)
            for t in range(2):
                V.tensor_reduce(kmax[:, t:t + 1], kabs[:, t, :], AX_X, ALU.max).then_inc(S["kmaxs"], 1)
            V.memset(v17_v[:, 1, :, :, D0], 1.0).then_inc(S["kmaxs"], 1)
            dve.wait_ge(S["kmaxs"], 3)
            on_pool("kmax")
            link(V.tensor_tensor(bound[:, :], kmax[:, :], qabs[:, :], ALU.mult))
            dve.sem_inc(S["kmax"], 1)
            dve.wait_ge(S["sums_ps"], 1)
            link(V.tensor_reduce(bsum[:, :], ps[:, 4, 0:2], AX_X, ALU.max))
            link(V.tensor_scalar(bsum[:, :], bsum[:, :], 0.99 * CLAMP, None, ALU.is_lt))
            link(V.tensor_scalar(clipf[:, :], bsum[0:1, :], -1.0, 1.0, ALU.mult, ALU.add))
            link(V.tensor_scalar(thr[:, 0:2], ps[:, 4, 2:4], 1.0 / (FF * C), EPS_LN, ALU.mult, ALU.add))
            link(V.tensor_scalar(thr[:, 2:4], thr[:, 0:2], -0.5, None, ALU.mult))
            link(V.tensor_scalar(thr[:, 0:2], thr[:, 0:2], 0.5, None, ALU.mult))
            link(V.tensor_scalar(cf[:, 0, 0:NSUP], ps[0:1, 4, 4:4 + NSUP], 1.0, None, ALU.min))
            dve.sem_inc(S["thr"], 1)
            clip = dve.value_load(clipf[0:1, 0:1], min_val=0, max_val=1)

            def value_tile(c, b, t, proj):
                dve.wait_ge(S["e0_proj"], proj)
                dve.wait_ge(S["e0_pv"], HALVES * c)
                V.tensor_copy(v17_v[:, b, t, :, 0:D0], ps[:, 7, 0:C].rearrange("p (h d) -> p h d", h=H)
                              ).then_inc(S["e0_v"], 1)

            dve.wait_ge(S["nm"], 2)

            def skip_table():
                link(V.memset(cf[:, 1, :], 0.0))
                for s in range(1, NSUP + 1):
                    link(V.tensor_tensor(cf[:, 1, s:s + 1], cf[:, 1, s - 1:s], cf[:, 0, s - 1:s], ALU.add))
                at = [1, NSUP, NSUP]
                number = con[0:1, K_DIST:K_DIST + NSUP]
                link(V.tensor_tensor(cq[:, 0:NSUP, :], cf[:, 1, 0:NSUP].unsqueeze(1).to_broadcast(at),
                                     number.unsqueeze(2).to_broadcast(at), ALU.is_equal))
                for row in (cf[:, 0, 0:NSUP], number):
                    link(V.tensor_tensor(cq[:, 0:NSUP, :], cq[:, 0:NSUP, :],
                                         row.unsqueeze(1).to_broadcast(at), ALU.mult))
                link(V.tensor_reduce(cf[:, 0, 0:NSUP], cq[:, 0:NSUP, :], AX_X, ALU.add))
                link(V.tensor_copy(sup[:, 0, 0:NSUP], cf[:, 0, 0:NSUP]))
                link(V.tensor_copy(sup[:, 1, :], cf[:, 1, :]))
                dve.sem_inc(S["skips"], 1)

            def unpack(s):
                link(V.tensor_scalar(enc[:, :, :], pk[:, :, :], 2 * s, 3, ALU.logical_shift_right,
                                     ALU.bitwise_and))
                link(V.tensor_scalar(wtf[:, :, 64 * s:64 * s + 64], enc[:, :, :], -1.0, fsc[:, 0:1], ALU.add,
                                     ALU.mult))

            def chunk0(c, b, nxt, side=False):
                for u in range(HALVES):
                    k = HALVES * c + u
                    if side and u == 0:
                        skip_table()
                        dve.wait_ge(S["ld_small"], 16 * 9)
                        link(V.tensor_scalar(neg[:, :], tri, 1.0, CLAMP, ALU.subtract, ALU.mult))
                        link(V.tensor_scalar(slp[:, 0:H], slp[:, 0:H], -1.0, None, ALU.mult))
                        link(V.tensor_scalar(nbg[:, :], nbg[:, :], -1.0, None, ALU.mult))
                        dve.sem_inc(S["nbg"], 1)
                    elif side and u in (1, 2, 3, 4):
                        unpack(u - 1)
                    z = u % 2
                    s = bank(2 * z, 2)
                    with dve.If(clip > 0):
                        dve.wait_ge(S["e0_score"], k + 29)
                        V.scalar_tensor_tensor(s, nm[:, 1024 * z:1024 * z + 1024], CLAMP, s, ALU.add, ALU.min
                                               ).then_inc(S["clip_min"], 1)
                        dve.wait_ge(S["clip_min"], k + 1)
                        V.scalar_tensor_tensor(s, nm[:, 1024 * z:1024 * z + 1024], -CLAMP, s, ALU.add, ALU.max
                                               ).then_inc(S["clip_max"], 1)
                        dve.wait_ge(S["clip_max"], k + 1)
                        dve.sem_inc(S["e0_ok"], 1)
                    with dve.Else():
                        dve.wait_ge(S["e0_score"], k + 29)
                        dve.sem_inc(S["e0_ok"], 1)
                    if nxt:
                        if u - 1 in KEYS_AT:
                            key_block_lo(c + 1, KEYS_AT.index(u - 1))
                        if u in VALUES_AT:
                            t = VALUES_AT.index(u)
                            value_tile(c + 1, 1 - b, t, 22 + 11 * (c + 1) + V_ORDER[t])

            with dve.Fori(0, NCH - 2, 2) as c:
                for b in range(2):
                    chunk0(c + b, b, True)
            chunk0(NCH - 2, 0, True, side=True)
            chunk0(NCH - 1, 1, False)

            dve.wait_ge(S["o0_q"], 1)
            dve.wait_ge(S["ld_rows"], 16 * 7)
            o4 = ps[:, 1, :].rearrange("p (a j r) -> p a j r", a=4, j=4)
            on4 = on[:, :].rearrange("p (a j d) -> p a j d", a=4, j=4)
            rl4 = rl[:, :].rearrange("p (a j) -> p a j", a=4)
            link(V.reciprocal(rl4, o4[:, :, :, D0]))
            link(V.tensor_tensor(on4, o4[:, :, :, 0:D0], rl4.unsqueeze(3).to_broadcast([P, 4, 4, D0]), ALU.mult))
            link(V.tensor_tensor(on[:, :], on[:, :], rows[:, R_BV0, :], ALU.add))
            dve.sem_inc(S["to_turn"], 1)
            dve.wait_ge(S["y"], 1)
            add_to_x(ps[:, 3, 0:C], R_BO0)

            normed("x1")
            dve.wait_ge(S["ga_exp"], 1)
            link(V.tensor_scalar(g1[:, 0:1], g1[:, 0:1], 1.0, None, ALU.add))
            link(V.reciprocal(g1[:, 1:2], g1[:, 0:1]))
            link(V.tensor_scalar(g1[:, 1:2], g1[:, 1:2], 1e-8, None, ALU.add))
            dve.sem_inc(S["ga_gate"], 1)
            dve.wait_ge(S["ga_log"], 1)
            dve.wait_ge(S["turned_sb"], turn("x1"))
            link(V.tensor_scalar(xn[:, T:2 * T], ones, g1[:, 2:3], None, ALU.mult))
            dve.sem_inc(S["ga_lgb"], 1)
            dve.wait_ge(S["ga_cum"], 1)
            link(V.tensor_copy(g1[:, 3:4], ps[:, 4, T:T + 1]))
            link(V.tensor_scalar(xn[:, 0:T], ps[:, 4, 0:T], g1[:, 3:4], 0.0, ALU.subtract, ALU.min))
            dve.sem_inc(S["ga_diff"], 1)
            dve.wait_ge(S["ga_decay"], 1)
            dve.wait_ge(S["ga_scores"], 1)
            link(V.tensor_tensor(xn[:, 0:T], xn[:, 0:T], tri, ALU.mult))
            link(V.scalar_tensor_tensor(xn[:, 0:T], ps[:, 5, 0:T], (M0 * T) ** -0.5, xn[:, 0:T], ALU.mult,
                                        ALU.mult))
            dve.sem_inc(S["ga_w"], 1)
            dve.wait_ge(S["y"], 2)
            add_to_x(ps[:, 7, 0:C])

            normed("x2")
            hT = v17[:, 2048:2048 + FF].rearrange("p (k t) -> p k t", k=8)
            for i in range(2):
                half = slice(4 * i, 4 * i + 4)
                dve.wait_ge(S["ff_h"], i + 1)
                link(V.tensor_tensor(hT[:, half], ps[:, 1 + i, :].rearrange("p (k t) -> p k t", k=4),
                                     b1c[:, half].unsqueeze(2).to_broadcast([P, 4, T]), ALU.add))
                V.tensor_scalar(hT[:, half], hT[:, half], 0.0, None, ALU.max).then_inc(S["ff_hsb"], 1)
            dve.wait_ge(S["y"], 3)
            add_to_x(ps[:, 3, 0:C], R_B2)

            layernorm("x3")
            link(V.bn_stats(st6[:, :], xn[:, :]))
            link(V.bn_aggr(mv[:, :], st6[:, :]))
            link(V.tensor_scalar(rstd[:, :], mv[:, 1:2], EPS_LN, None, ALU.add))
            on_pool("rstd")
            link(V.tensor_scalar(xn[:, :], xn[:, :], mv[:, 0:1], rstd[:, 0:1], ALU.subtract, ALU.mult))
            link(V.tensor_tensor(xn[:, :], xn[:, :], rows[:, R_GAM, :], ALU.mult))
            link(V.tensor_tensor(xn[:, :], xn[:, :], rows[:, R_BET, :], ALU.add))
            dve.sem_inc(S["to_turn"], 1)
            dve.wait_ge(S["wv1_hi"], 1)
            V.tensor_tensor(wv1[:, W_AL, :], wv1raw[:, 0, :], wv1[:, W_AH, :].bitcast(F32), ALU.subtract)
            V.tensor_tensor(wv1[:, W_BL, :], wv1raw[:, 1, :], wv1[:, W_BH, :].bitcast(F32), ALU.subtract
                            ).then_inc(S["wv1_lo"], 1)
            dve.wait_ge(S["qa_hi"], 1)
            V.tensor_tensor(asp[:, 1, :], bank(0, 4), asp[:, 0, :].bitcast(F32), ALU.subtract
                            ).then_inc(S["qa_lo"], 1)
            dve.wait_ge(S["qb_hi"], 1)
            V.tensor_tensor(asp[0:64, 3, :], bank(4, 4)[0:64, :], asp[0:64, 2, :].bitcast(F32), ALU.subtract
                            ).then_inc(S["qb_lo"], 1)
            link(V.memset(mx[:, :], -3.0e38))

            total = dve.value_load(sup[0:1, 1, NSUP:NSUP + 1], min_val=0, max_val=NSUP)
            with dve.Fori(0, NSUP) as n:
                with dve.If(total - n > 0):
                    for b in range(2):
                        g = 2 * n + b
                        dve.wait_ge(S["m1_negm"], g + 3)
                        dve.wait_ge(S["m1_merge"], g + 1)
                        for h in range(H):
                            dve.wait_ge(S["m1_head"], H * g + h + 33)
                            dve.wait_ge(S["m1_red"], H * g + h + 31)
                            V.memset(pause2[:, h % 2:h % 2 + 1], 0.0)
                            nc.vector.tensor_tensor_reduce(
                                out=junk[:, h % 2],
                                in0=ps[:, 2 * (h % 2):2 * (h % 2) + 2, 0:NB],
                                in1=negm[:, b, :].bitcast(F32).rearrange("p (j n) -> p j n", j=2),
                                scale=1.0, scalar=-3.0e38, op0=ALU.add, op1=ALU.max,
                                accum_out=cm[:, h:h + 1]).then_inc(S["m1_red"], 1)
                        dve.wait_ge(S["m1_red"], H * g + H + 32)
                        V.tensor_tensor(mx[:, :], mx[:, :], cm[:, :], ALU.max).then_inc(S["m1_merge"], 1)
            dve.wait_ge(S["m1_merge"], 2 * total + 1)
            minus_max("m1_ml")
            dve.sem_inc(S["m1_end"], 1)

            def mask_and_sum(k, b, u):
                sl = pr[:, (HALVES * b + u) % 4, :].rearrange("p (h q) -> p h q", h=8)
                acc = nm[:, 1024 * (u % 2):1024 * (u % 2) + 1024]
                dve.wait_ge(S["e1_exp"], k + 3)
                V.tensor_tensor(sl, sl, mk[:, b, u // 2, :].unsqueeze(1).to_broadcast([P, 8, T]), ALU.mult
                                ).then_inc(S["e1_masked"], 1)
                dve.wait_ge(S["e1_masked"], k + 29)
                dve.wait_ge(S["e1_sum"], k + 4)
                V.tensor_tensor(acc, acc, pr[:, (HALVES * b + u) % 4, :], ALU.add).then_inc(S["e1_sum"], 1)

            dve.wait_ge(S["sums_zero"], 1)
            with dve.Fori(0, NSUP) as n:
                with dve.If(total - n > 0):
                    for b in range(2):
                        g = 2 * n + b
                        for u in range(HALVES):
                            k = HALVES * g + u
                            if u == 0:
                                dve.wait_ge(S[f"e1_mask{b}"], 16 * n + 16)
                            dve.wait_ge(S["e1_score"], k + 3)
                            V.tensor_scalar(bank(2 * (u % 2), 2), bank(2 * (u % 2), 2), 80.0, None, ALU.min
                                            ).then_inc(S["e1_ok"], 1)
                            if (b, u) != (0, 0):
                                mask_and_sum(k - 1, (b - (u == 0)) % 2, (u - 1) % HALVES)
                    mask_and_sum(HALVES * (2 * n + 1) + HALVES - 1, 1, HALVES - 1)
            dve.wait_ge(S["e1_sum"], 2 * HALVES * total + 4)
            steps[0] += 1
            V.memset(st6[:, :], 0.0).then_inc(S["dve_step"], 1)
            dve.wait_ge(S["dve_step"], steps[0])
            dve.sem_inc(S["e1_sums"], 1)
            dve.wait_ge(S["o1_ps"], 1)
            for k in range(4):
                part = slice(256 * k, 256 * k + 256)
                link(V.reciprocal(pr[:, 0, part], bank(0, 2)[:, part]))
                V.tensor_tensor(pr[:, 1, part], bank(4, 2)[:, part], pr[:, 0, part], ALU.mult
                                ).then_inc(S["o1"], 1)
            dve.wait_ge(S["y"], 4)
            add_to_x(ps[:, 6, 0:C], R_BO1)

            sc = pr_flat[:, 0:HQ]
            sd = pr_flat[:, HQ:2 * HQ]
            xn2 = on[:, 0:T]
            sc3 = sc.rearrange("p (h q) -> p h q", h=H)
            sd3 = sd.rearrange("p (h q) -> p h q", h=H)
            normed("x4")
            link(V.memset(v17[:, 0:H * 17].rearrange("p (h d) -> p h d", h=H)[:, :, D0], 1.0))
            link(V.tensor_tensor(xn2, dist, tri, ALU.mult))
            for h in range(H):
                last = V.scalar_tensor_tensor(sd3[:, h], xn2, slp[:, h:h + 1], neg[:, :], ALU.mult,
                                              ALU.add)
            link(last)
            dve.wait_ge(S["sa_proj"], 1)
            for t in range(2):
                link(V.tensor_scalar(xn[:, t * T:(t + 1) * T], ps[:, 3, t * T:(t + 1) * T], 4.0, None, ALU.mult))
                V.tensor_tensor(nm[:, 1024 * t:1024 * t + 1024].rearrange("p (h q) -> p h q", h=8),
                                     xn[:, t * T:(t + 1) * T].unsqueeze(1).to_broadcast([P, 8, T]),
                                     con[:, K_HEAD:K_HEAD + 8].unsqueeze(2).to_broadcast([P, 8, T]), ALU.mult
                                ).then_inc(S["sa_q"], 1)
            for k in range(2):
                half = slice(1024 * k, 1024 * k + 1024)
                kept8 = tri.unsqueeze(1).to_broadcast([P, 8, T])
                dve.wait_ge(S["sa_scores"], k + 1)
                link(V.tensor_tensor(sc3[:, 8 * k:8 * k + 8], bank(4 + 2 * k, 2).rearrange(
                    "p (h q) -> p h q", h=8), kept8, ALU.mult))
                link(V.tensor_tensor(sc[:, half], sc[:, half], sd[:, half], ALU.add))
                link(V.scalar_tensor_tensor(sd[:, half], sc[:, half], -1.0, sc[:, half], ALU.mult, ALU.max))
                link(V.tensor_scalar(sd[:, half], sd[:, half], 1.0, None, ALU.add))
                link(V.reciprocal(sd[:, half], sd[:, half]))
                link(V.tensor_tensor(sc[:, half], sc[:, half], sd[:, half], ALU.mult))
                link(V.tensor_scalar(sc[:, half], sc[:, half], -0.99999994, None, ALU.max))
                dve.sem_inc(S["sa_soft"], 1)
            dve.wait_ge(S["sa_pv"], 1)
            o17 = ps[:, 3, 0:H * 17].rearrange("p (h d) -> p h d", h=H)
            link(V.tensor_scalar(rl[:, :], o17[:, :, D0], 1e-6, None, ALU.add))
            link(V.reciprocal(rl[:, :], rl[:, :]))
            link(V.tensor_tensor(on[:, :].rearrange("p (h d) -> p h d", h=H), o17[:, :, 0:D0],
                                 rl[:, :].unsqueeze(2).to_broadcast([P, H, D0]), ALU.mult))
            dve.sem_inc(S["to_turn"], 1)
            dve.wait_ge(S["y"], 5)
            add_to_x(ps[:, 1, 0:C])

            magic = 12582912.0
            layernorm("x5")
            link(V.tensor_reduce(rstd[:, :], xn[:, :], AX_X, ALU.max, apply_absolute_value=True))
            link(V.tensor_scalar(rstd[:, :], rstd[:, :], 1e-5, None, ALU.max))
            link(V.reciprocal(rstd[:, :], rstd[:, :]))
            link(V.tensor_scalar(rstd[:, :], rstd[:, :], 127.0, None, ALU.mult))
            link(V.tensor_scalar(xn[:, :], xn[:, :], rstd[:, 0:1], None, ALU.mult))
            link(V.tensor_scalar(xn[:, :], xn[:, :], magic, magic, ALU.add, ALU.subtract))
            link(V.tensor_scalar(xn[:, :], xn[:, :], 127.0, -128.0, ALU.min, ALU.max))
            link(V.reciprocal(rstd[:, :], rstd[:, :]))
            link(V.tensor_scalar(xn[:, :], xn[:, :], rstd[:, 0:1], None, ALU.mult))
            dve.sem_inc(S["to_turn"], 1)
            dve.wait_ge(S["y"], 6)
            add_to_x(ps[:, 3, 0:C], R_FB)
            dve.sem_inc(S["x_done"], 1)

        @block.tensor
        def _(pe):
            mm = nc.tensor.matmul

            pe.sem_inc(S["m0_proj"], 8)
            pe.sem_inc(S["m0_head"], 32)
            pe.sem_inc(S["e0_proj"], 22)
            pe.sem_inc(S["e0_score"], 28)
            pe.sem_inc(S["e0_pv"], 14)
            pe.sem_inc(S["m1_head"], 32)
            pe.sem_inc(S["e1_score"], 2)
            pe.sem_inc(S["e1_pv"], 4)
            pe.sem_inc(S["e1_chunk"], 2)

            def transposes(tag, src, b=0):
                pe.wait_ge(S["to_turn"], turn(tag))
                for k in range(2):
                    last = nc.tensor.transpose(ps[:, b, k * T:(k + 1) * T], src[:, k * P:(k + 1) * P], ident)
                last.then_inc(S["turned"], 1)

            def from_xT(dst, xT, w, name):
                for k in range(2):
                    last = mm(dst, xT[:, k, :], w[:, k, :], start=(k == 0), stop=(k == 1))
                last.then_inc(S[name], 1)

            pe.wait_ge(S["ld_con"], 16)
            transposes("x0", xn)
            pe.wait_ge(S["turned_sb"], turn("x0"))
            pe.wait_ge(S["ld_wq0"], 32)
            for t in range(2):
                dst = ps[:, 4, t * T:(t + 1) * T]
                for k in range(2):
                    mm(dst, wq0[:, k, t * P:(t + 1) * P], xnT[:, k, :], start=(k == 0), stop=False)
                last = mm(dst, wq0[0:1, 2, t * P:(t + 1) * P], ones[0:1, :], start=False, stop=True)
            last.then_inc(S["qs_ps"], 1)

            def project_max0(c, b, blocks=range(4)):
                if 0 in blocks:
                    pe.wait_ge(S["m0_split"], c + 1)
                for i in blocks:
                    t, n = i // 2, i % 2
                    pe.wait_ge(S["m0_keys"], 4 * c + i + 3)
                    dst = ps[:, 4 + i % 2, 0:NB]
                    mm(dst, wk0[:, W_AH, t * P:(t + 1) * P], ct[:, b, X_AH, n * NB:(n + 1) * NB],
                       start=True, stop=False)
                    mm(dst, wk0[0:64, W_BH, t * P:(t + 1) * P], ct[0:64, b, X_B, n * NB:(n + 1) * NB],
                       start=False, stop=True).then_inc(S["m0_proj"], 1)

            def heads_max0(c, b, heads, last_chunk=False):
                for h in heads:
                    t = h // 8
                    if h % 8 == 0:
                        pe.wait_ge(S["m0_keys"], 4 * c + 2 * t + 6)
                    bank = head_bank(b, h)
                    back, user = last_user(b, h)
                    if last_chunk:
                        bank = 2 * (h % 2)
                        back, user = (0, h - 2) if h > 1 else (-1, {0: H - 1, 1: H - 3}[h])
                    pe.wait_ge(S["m0_staged" if user % 2 else "m0_red"],
                               8 * (c + back) + user // 2 + 1 + 8)
                    for n in range(2):
                        last = mm(ps[:, bank + n, 0:NB], qn[:, h, :],
                                  kn[:, b, t, n * NB:(n + 1) * NB], start=True, stop=True)
                    last.then_inc(S["m0_head"], 1)

            pe.wait_ge(S["w0_hi"], 1)
            pe.wait_ge(S["qn"], 1)
            project_max0(0, 0)

            def chunk_max0(c, b):
                for i in range(4):
                    heads_max0(c, b, range(3 * i, 3 * i + 3))
                    project_max0(c + 1, 1 - b, [i])
                heads_max0(c, b, range(12, H))

            with pe.Fori(0, NCH - 2, 2) as c:
                for b in range(2):
                    chunk_max0(c + b, b)
            chunk_max0(NCH - 2, 0)
            def project0(c, b, i):
                t, n = i // 2, i % 2
                if i == 0:
                    pe.wait_ge(S["e0_lo"], c + 2)
                pe.wait_ge(S["e0_klo"], 4 * c + i + 1)
                dst = ps[:, 5 + i % 2, 0:NB]
                for j, (w, xx) in enumerate(PAIRS):
                    last = mm(dst, wk0[:, w, t * P:(t + 1) * P], ct[:, b, xx, n * NB:(n + 1) * NB],
                              start=(j == 0), stop=(j == 4))
                last.then_inc(S["e0_proj"], 1)

            def values0(c, b, t, bank=7, emptied=1):
                pe.wait_ge(S["e0_v"], TPC * c + t + emptied)
                for j, (w, xx) in enumerate(PAIRS):
                    last = mm(ps[:, bank, 0:C], ct[:, b, xx, t * P:(t + 1) * P], wv0[:, w, :],
                              start=(j == 0), stop=(j == 4))
                last.then_inc(S["e0_proj"], 1)

            def scores0(c, b, u):
                z, t = u % 2, u // 2
                pe.wait_ge(S["e0_exp"], HALVES * c + u + 1)
                for k in range(4):
                    gg = 4 * z + k
                    last = mm(ps[:, 2 * z + k // 2, (k % 2) * 256:(k % 2) * 256 + 256],
                              ks_v[:, b, gg, t * P:(t + 1) * P], qs[:, gg * 256:gg * 256 + 256],
                              start=True, stop=True)
                last.then_inc(S["e0_score"], 1)

            def weigh0(c, b, u):
                z, t = u % 2, u // 2
                pe.wait_ge(S["e0_exp"], HALVES * c + u + 3)
                pe.wait_ge(S["e0_v"], TPC * c + t + 2)
                for k in range(8):
                    h = 8 * z + k
                    j = h % 4
                    last = mm(ps[32 * j:32 * j + 17, 4, (h // 4) * T:(h // 4 + 1) * T],
                              v17_v[:, b, t, h, :], pr[:, (HALVES * b + u) % 4, k * T:(k + 1) * T],
                              start=False, stop=True, skip_group_check=True)
                last.then_inc(S["e0_pv"], 1)

            pe.wait_ge(S["w0_lo"], 1)
            for h in range(H):
                heads_max0(NCH - 1, 1, [h], last_chunk=True)
                if h == 1:
                    pe.wait_ge(S["m0_keys"], 4 * NCH + 4)
                    pe.wait_ge(S["m0_red"], 8 * (NCH - 1) + 8)
                if h in (1, 3, 5, 7):
                    project0(0, 0, h // 2)
                if h >= 8 and h - 8 < TPC:
                    t = h - 8
                    values0(0, 0, t, bank=7 if t % 2 == 0 else 4, emptied=1 if t == 0 else 0)

            pe.wait_ge(S["m0_ml"], 1)
            for h in range(H):
                last = mm(ps[96:P, h // 4, (h % 4) * T:(h % 4 + 1) * T], ml[:, h, :], ident,
                          start=True, stop=True)
            last.then_inc(S["m0_row"], 1)
            pe.wait_ge(S["selr"], 1)
            pe.wait_ge(S["qs_max"], 1)
            pe.wait_ge(S["qs_rows"], 192)
            for k in range(4):
                last = mm(ps[:, k, :], selr[:, :], qs[:, 512 * k:512 * k + 512], start=True, stop=True)
                if k % 2 == 1:
                    last.then_inc(S["nm_row"], 1)
            pe.wait_ge(S["kmax"], 1)
            pe.wait_ge(S["mask_sum"], NSUP)
            mm(ps[:, 4, 4:4 + NSUP], ones, cnt[:, 0:NSUP], start=True, stop=True)
            mm(ps[:, 4, 0:2], ones, bound[:, :], start=True, stop=True)
            pe.wait_ge(S["wsum"], 2)
            mm(ps[:, 4, 2:4], ones, wsum[:, :], start=True, stop=True).then_inc(S["sums_ps"], 1)
            pe.wait_ge(S["nm"], 1)
            pe.wait_ge(S["ks_ones"], 1)
            pe.wait_ge(S["e0_keys0"], 192)
            scores0(0, 0, 0)

            def step0(c, b, u, nxt, last):
                if u + 1 < HALVES:
                    scores0(c, b, u + 1)
                elif not last:
                    scores0(c + 1, 1 - b, 0)
                if nxt and u in KEYS_AT:
                    project0(c + 1, 1 - b, KEYS_AT.index(u))
                if nxt and u in VALUES_AT:
                    values0(c + 1, 1 - b, VALUES_AT.index(u))
                if u > 0:
                    weigh0(c, b, u - 1)

            def round0(c, b, i2, nxt):
                for u in range(1, HALVES - 1):
                    step0(c, b, u, True, False)
                pe.wait_ge(S["ks_ones"], 2)
                pe.wait_ge(S[f"e0_keys{1 - b}"], 192 * (i2 + 1 + b))
                step0(c, b, HALVES - 1, True, False)
                step0(c + 1, 1 - b, 0, nxt, False)
                weigh0(c, b, HALVES - 1)

            pe.wait_ge(S["nm"], 2)
            step0(0, 0, 0, True, False)
            pe.wait_ge(S["zero"], 1)
            pe.wait_ge(S["thr"], 1)
            mm(ps[:, 4, :], zero[:, 0:P], zero[:, :], start=True, stop=True)
            with pe.Fori(0, (NCH - 2) // 2) as i2:
                for b in range(2):
                    round0(2 * i2 + b, b, i2, True)
            round0(NCH - 2, 0, NSUP - 1, False)
            for u in range(1, HALVES):
                step0(NCH - 1, 1, u, False, True)
            weigh0(NCH - 1, 1, HALVES - 1)

            pe.wait_ge(S["o0_read"], 1)
            for k in range(4):
                last = nc.tensor.transpose(ps[:, 1, k * T:(k + 1) * T], oacc[:, k, :], ident)
            last.then_inc(S["o0_q"], 1)
            transposes("o0", on)
            pe.wait_ge(S["turned_sb"], turn("o0"))
            pe.wait_ge(S["ld_small"], 16 * 9)
            from_xT(ps[:, 3, 0:C], onT, wo0, "y")

            transposes("x1", xn)
            pe.wait_ge(S["turned_sb"], turn("x1"))
            for k in range(2):
                mm(ps[:, 1, 0:M0 + 1], xnT[:, k, :], a0w[:, k, 0:M0 + 1], start=(k == 0), stop=(k == 1))
            for j in range(2):
                for k in range(2):
                    last = mm(ps[0:M0, 2, j * T:(j + 1) * T],
                              a0w[:, k, M0 + 1 + j * M0:M0 + 1 + (j + 1) * M0], xnT[:, k, :],
                              start=(k == 0), stop=(k == 1))
            last.then_inc(S["ga_proj"], 1)
            pe.wait_ge(S["ga_kvq"], 1)
            mm(ps[:, 5, 0:T], onT[0:M0, 0, :], onT[0:M0, 1, :], start=True, stop=True
               ).then_inc(S["ga_scores"], 1)
            pe.wait_ge(S["ga_lgb"], 1)
            mm(ps[:, 4, 0:T], xn[:, T:2 * T], tri, start=True, stop=True)
            mm(ps[:, 4, T:T + 1], tri, g1[:, 2:3], start=True, stop=True).then_inc(S["ga_cum"], 1)
            pe.wait_ge(S["ga_w"], 1)
            mm(ps[0:M0, 6, 0:T], on[:, 0:M0], xn[:, 0:T], start=True, stop=True).then_inc(S["ga_reads"], 1)
            pe.wait_ge(S["ga_reads_sb"], 1)
            mm(ps[:, 7, 0:C], onT[0:M0, 0, :], a0wo[:, :], start=True, stop=True).then_inc(S["y"], 1)

            transposes("x2", xn)
            pe.wait_ge(S["turned_sb"], turn("x2"))
            pe.wait_ge(S["tern"], 12)
            for n in range(8):
                for k in range(2):
                    last = mm(ps[:, 1 + n // 4, (n % 4) * T:(n % 4 + 1) * T], ffw1[:, k, n * P:(n + 1) * P],
                              xnT[:, k, :], start=(k == 0), stop=(k == 1))
                if n % 4 == 3:
                    last.then_inc(S["ff_h"], 1)
            for n in range(8):
                if n % 4 == 0:
                    pe.wait_ge(S["ff_hsb"], n // 4 + 1)
                last = mm(ps[:, 3, 0:C], v17[:, 2048 + n * T:2048 + (n + 1) * T], ffw2[:, n, :],
                          start=(n == 0), stop=(n == 7))
            last.then_inc(S["y"], 1)

            transposes("x3", xn)
            pe.wait_ge(S["turned_sb"], turn("x3"))
            pe.wait_ge(S["ld_w1"], 32)
            for n in range(8):
                for k in range(2):
                    last = mm(ps[:, 1 + n // 4, (n % 4) * T:(n % 4 + 1) * T], wq1[:, k, n * P:(n + 1) * P],
                              xnT[:, k, :], start=(k == 0), stop=(k == 1))
                if n % 4 == 3:
                    last.then_inc(S["q1_ps"], 1)
            pe.wait_ge(S["q1"], 2)
            for e in range(2):
                for w, name in ((0, "qa_ps"), (1, "qb_ps")):
                    for h in range(e, H, 2):
                        last = mm(ps[:, 4 * w + h // 4, (h % 4) * T:(h % 4 + 1) * T],
                                  wkt[64 * e:64 * e + 64, h // 2, w * P:(w + 1) * P],
                                  q1[64 * e:64 * e + 64, (h // 2) * T:(h // 2 + 1) * T],
                                  start=True, stop=True)
                    if e == 1:
                        last.then_inc(S[name], 1)
                if e == 0:
                    last.then_inc(S["even_heads"], 1)
                    pe.wait_ge(S["even_heads"], 1)

            pe.wait_ge(S["qa_lo"], 1)
            for k in range(WARM_UP):
                mm(ps[:, k % 4, :], zero[:, 0:P], zero[:, :], start=True, stop=True)
            pe.wait_ge(S["qb_lo"], 1)
            pe.wait_ge(S["skips"], 1)
            total = pe.value_load(sup[0:1, 1, NSUP:NSUP + 1], min_val=0, max_val=NSUP)
            with pe.Fori(0, NSUP) as n:
                with pe.If(total - n > 0):
                    for b in range(2):
                        g = 2 * n + b
                        pe.wait_ge(S["m1_split"], g + 2)
                        for h in range(H):
                            pe.wait_ge(S["m1_red"], H * g + h + 31)
                            for j in range(2):
                                dst = ps[:, 2 * (h % 2) + j, 0:NB]
                                mm(dst, asp[:, 0, h * T:(h + 1) * T], ct[:, b, X_AH, j * NB:(j + 1) * NB],
                                   start=True, stop=False)
                                last = mm(dst, asp[0:64, 2, h * T:(h + 1) * T],
                                          ct[0:64, b, X_B, j * NB:(j + 1) * NB], start=False, stop=True)
                            last.then_inc(S["m1_head"], 1)

            pe.wait_ge(S["m1_ml"], 1)
            for h in range(H):
                last = mm(ps[64:96, h // 4, (h % 4) * T:(h % 4 + 1) * T], ml[:, h, :], ident,
                          start=True, stop=True)
            last.then_inc(S["m1_row"], 1)
            for k in (4, 5):
                mm(ps[:, k, :], zero[:, 0:P], zero[:, :], start=True, stop=True)

            def scores1(g, b, u):
                z, t = u % 2, u // 2
                pe.wait_ge(S["e1_exp"], HALVES * g + u + 1)
                passes = [(ct[:, b, X_AH], 0), (ct[:, b, X_AH], 1), (ct[:, b, X_AL], 0), (ct[:, b, X_B], 2)]
                for j in range(2):
                    cols = slice(1024 * z + 512 * j, 1024 * z + 512 * j + 512)
                    for i, (xx, w) in enumerate(passes):
                        mm(ps[:, 2 * z + j, :], xx[:, t * P:(t + 1) * P], asp[:, w, cols],
                           start=(i == 0), stop=False)
                    last = mm(ps[:, 2 * z + j, :], x5[0:96, b, t * P:(t + 1) * P], asp[0:96, 3, cols],
                              start=False, stop=True)
                last.then_inc(S["e1_score"], 1)

            def values1(g, b, t):
                pe.wait_ge(S["e1_v"], TPC * g + t + 1)
                for j in range(2):
                    for i, (w, xx) in enumerate(PAIRS):
                        last = mm(ps[:, 6 + j, :], ct[:, b, xx, t * P:(t + 1) * P],
                                  wv1[:, w, 512 * j:512 * j + 512], start=(i == 0), stop=(i == 4))
                last.then_inc(S["e1_vps"], 1)

            def weigh1(g, b, u):
                z, t = u % 2, u // 2
                pe.wait_ge(S["e1_masked"], HALVES * g + u + 29)
                pe.wait_ge(S["e1_v"], TPC * g + t + 2)
                for k in range(8):
                    h = 8 * z + k
                    e = 64 * (h % 2)
                    last = mm(ps[e:e + 64, 4 + z, ((h // 2) % 4) * T:((h // 2) % 4 + 1) * T],
                              v1[:, (TPC * b + t) % 2, h * D1:(h + 1) * D1],
                              pr[:, (HALVES * b + u) % 4, k * T:(k + 1) * T],
                              start=False, stop=True, skip_group_check=True)
                last.then_inc(S["e1_pv"], 1)
                return last

            pe.wait_ge(S["a5_max"], 1)
            pe.wait_ge(S["x5_ones"], 1)
            pe.wait_ge(S["wv1_lo"], 1)
            with pe.Fori(0, NSUP) as n:
                with pe.If(total - n > 0):
                    pe.wait_ge(S["e1_split"], 2 * n + 2)
                    scores1(2 * n, 0, 0)
                    values1(2 * n, 0, 0)
                    for i in range(2 * HALVES + 1):
                        if i + 1 < 2 * HALVES:
                            b1, u1 = (i + 1) // HALVES, (i + 1) % HALVES
                            if u1 == 0:
                                pe.wait_ge(S["e1_split"], 2 * n + 3)
                            scores1(2 * n + b1, b1, u1)
                            if u1 % 2 == 0:
                                values1(2 * n + b1, b1, u1 // 2)
                        if i == 0:
                            continue
                        b, u = (i - 1) // HALVES, (i - 1) % HALVES
                        weigh1(2 * n + b, b, u)
                        if u == HALVES - 1:
                            pe.wait_ge(S["e1_pv"], HALVES * (2 * n + b) + HALVES + 4)
                            pe.sem_inc(S["e1_chunk"], 1)

            pe.wait_ge(S["e1_sums"], 1)
            for h in range(H):
                e, k = 64 * (h % 2), h // 2
                last = mm(ps[e:e + 64, k // 4, (k % 4) * T:(k % 4 + 1) * T], ones[:, 0:64],
                          nm[:, h * T:(h + 1) * T], start=True, stop=True)
            last.then_inc(S["o1_ps"], 1)
            pe.wait_ge(S["ld_wo1"], 16)
            for n in range(8):
                if n % 2 == 0:
                    pe.wait_ge(S["o1"], n // 2 + 1)
                last = mm(ps[:, 6, 0:C], pr[:, 1, n * T:(n + 1) * T], wo1[:, n, :], start=(n == 0), stop=(n == 7))
            last.then_inc(S["y"], 1)

            transposes("x4", xn)
            pe.wait_ge(S["turned_sb"], turn("x4"))
            pe.wait_ge(S["ld_aw"], 16)
            for w, b in ((0, 3), (1, 1)):
                for t in range(2):
                    for k in range(2):
                        mm(ps[:, b, t * T:(t + 1) * T], aw[:, w, k, t * P:(t + 1) * P], xnT[:, k, :],
                           start=(k == 0), stop=(k == 1))
            from_xT(ps[:, 2, 0:C], xnT, aw[:, 2], "sa_proj")
            pe.wait_ge(S["sa_kv"], 1)
            for k in range(4):
                if k % 2 == 0:
                    pe.wait_ge(S["sa_q"], k // 2 + 1)
                last = mm(ps[:, 4 + k, :], onT[:, k // 2, :], nm[:, 512 * k:512 * k + 512], start=True, stop=True)
                if k % 2 == 1:
                    last.then_inc(S["sa_scores"], 1)
            for h in range(H):
                if h % 8 == 0:
                    pe.wait_ge(S["sa_exp"], h // 8 + 1)
                last = mm(ps[:, 3, h * 17:(h + 1) * 17], pr_flat[:, h * T:(h + 1) * T],
                          v17[:, h * 17:(h + 1) * 17], start=True, stop=True)
            last.then_inc(S["sa_pv"], 1)
            transposes("o4", on)
            pe.wait_ge(S["turned_sb"], turn("o4"))
            from_xT(ps[:, 1, 0:C], onT, aw[:, 3], "y")

            transposes("x5", xn)
            pe.wait_ge(S["turned_sb"], turn("x5"))
            from_xT(ps[:, 3, 0:C], xnT, wtf, "y")


def kernel(**inputs):
    import concourse.bacc as bacc
    from concourse.bass_utils import run_bass_kernel_spmd

    def at(name):
        return np.asarray(inputs[name])

    def row(v):
        return v.reshape(1, -1)

    def padded(w):
        return np.concatenate([w, w[P:CKV]], axis=0)

    mask = at("mask_1x1xSxS2_bk0")[0, 0]
    wkv1 = at("L1_xattn_Wkv")
    wk1t = wkv1[:, :INNER].T
    where = np.arange(P)
    feed = {
        "x": at("x")[0],
        "ctxT": at("ctx_768")[0].T,
        "mask_q": np.ascontiguousarray(mask).view(np.int32),
        "mask_k": np.ascontiguousarray(mask.T).view(np.int32),
        "Wq0": at("L0_xattn_Wq"), "bq0": row(at("L0_xattn_bq")),
        "Wk0": padded(at("L0_xattn_Wk")), "Wv0": padded(at("L0_xattn_Wv")),
        "bk0": at("L0_xattn_bk").reshape(2, P).T,
        "bv0": row(at("L0_xattn_bv")), "bo0": row(at("L0_xattn_bo")), "b2": row(at("L0_ffn_b2")),
        "gamma": row(at("L1_xattn_ln_gamma")), "beta": row(at("L1_xattn_ln_beta")),
        "bo1": row(at("L1_xattn_bo")), "fbias": row(at("L1_ffn_bias")),
        "Wo0": at("L0_xattn_Wo"),
        "A0": np.concatenate([at("L0_attn_Wk").T, at("L0_attn_Wg").T, at("L0_attn_Wv").T,
                              at("L0_attn_Wq").T], axis=1),
        "A0o": at("L0_attn_Wo").T, "bg": row(at("L0_attn_bg")),
        "b1": at("L0_ffn_b1").reshape(FF // P, P).T,
        "W1T": at("L0_ffn_W1").T, "W2T": at("L0_ffn_W2").T,
        "slopes": row(at("L1_attn_alibi_slopes")), "power": row(at("L1_attn_power")),
        "fscale": row(at("L1_ffn_weight_scale")),
        "packed": at("L1_ffn_packed_weight").reshape(64, C).T,
        "Wq1": at("L1_xattn_Wq"),
        "Wkt1": np.concatenate([wk1t, wk1t[:, P:CKV]], axis=1),
        "Wv1": padded(wkv1[:, INNER:]),
        "Wo1": at("L1_xattn_Wo"),
        "A1": np.concatenate([at("L1_attn_Wq").T, at("L1_attn_Wk").T, at("L1_attn_Wv").T,
                              at("L1_attn_Wo").T], axis=0),
        "constants": np.concatenate([
            where[:, None] == where[None, :], where[:, None] <= where[None, :], np.ones((P, P)),
            np.abs(where[:, None] - where[None, :]), np.repeat(where[:, None] >= 96, P, axis=1),
            where[:, None] // D0 == np.arange(8)[None, :],
            where[:, None] // D0 % 2 == np.arange(2)[None, :]], axis=1).astype(np.float32),
    }
    feed = {k: np.ascontiguousarray(v) for k, v in feed.items()}
    nc = bacc.Bacc("TRN2", target_bir_lowering=False, num_devices=1)
    a = {k: nc.dram_tensor("in_" + k, v.shape, mybir.dt.from_np(v.dtype), kind="ExternalInput").ap()
         for k, v in feed.items()}
    out = nc.dram_tensor("out", (1, T, C), F32, kind="ExternalOutput").ap()
    perceiver(nc, a, out[0])
    r = run_bass_kernel_spmd(nc, [{"in_" + k: v for k, v in feed.items()}], core_ids=[0])
    return r.results[0]["out"]
```
